# Optimizing a Trainium2 kernel written in Bass

```python
import numpy as np
import jax
import jax.numpy as jnp

def _softmax(x, axis=-1):
    return jax.nn.softmax(x, axis=axis)

def _gelu(x):
    return jax.nn.gelu(x, approximate=True)

def _silu(x):
    return jax.nn.silu(x)

def _sigmoid(x):
    return jax.nn.sigmoid(x)

def _layernorm(x, axis=-1, eps=1e-05):
    m = jnp.mean(x, axis=axis, keepdims=True)
    v = jnp.var(x, axis=axis, keepdims=True)
    return (x - m) / jnp.sqrt(v + eps)

def _scatter_add(tgt, idx, src, axis=0):
    return tgt.at[idx].add(src)

def _segment_sum(src, seg, n):
    return jax.ops.segment_sum(src, seg, n)
kernel_name = 'mk_gnn_resnorm_d1_gnn_r8_5285e3'

def setup_inputs(seed: int=0):
    np.random.seed(seed)
    _w = jnp.asarray

    def _rec_inputs():
        import jax
        import jax.numpy as jnp
        _gk = jax.random.key(seed)
        x = -0.000202 + 1 * jax.random.normal(jax.random.fold_in(_gk, 1), (6250, 128), jnp.float32)
        src = jax.random.randint(jax.random.fold_in(_gk, 2), (200000,), 0, 6250, jnp.int32)
        dst = jnp.minimum((6250 * jax.random.uniform(jax.random.fold_in(_gk, 3), (200000,)) ** 2.0).astype(jnp.int32), 49999)
        _o = jnp.argsort(dst, stable=True)
        src = src[_o]
        dst = dst[_o]
        return (x, src, dst)
    x, src, dst = _rec_inputs()

    def _L0_gnn_setup():
        import jax, jax.numpy as jnp
        import numpy as np
        LN_EPS = 1e-05
        N_NODES = 6250
        IN_DIM = 128
        OUT_DIM = 128
        N_EDGES = 100000

        def _ln(x, g, b):
            m = jnp.mean(x, axis=-1, keepdims=True)
            v = jnp.mean((x - m) ** 2, axis=-1, keepdims=True)
            return (x - m) * jax.lax.rsqrt(v + LN_EPS) * g + b
        key = jax.random.key(seed)
        ks = jax.random.split(key, 16)

        def lin(k, fan_in, fan_out):
            return jax.random.normal(k, (fan_in, fan_out), dtype=jnp.float32) / np.sqrt(fan_in)
        x = jax.random.normal(ks[0], (N_NODES, IN_DIM), dtype=jnp.float32)
        edge_index = jax.random.randint(ks[1], (2, N_EDGES), 0, N_NODES, dtype=jnp.int64)
        return {'x': x, 'edge_index': edge_index, 'W1': lin(ks[2], IN_DIM, OUT_DIM), 'b1': jnp.zeros((OUT_DIM,), jnp.float32), 'g1': jnp.ones((OUT_DIM,), jnp.float32), 'bt1': jnp.zeros((OUT_DIM,), jnp.float32), 'We1': lin(ks[3], 2 * OUT_DIM, OUT_DIM), 'be1': jnp.zeros((OUT_DIM,), jnp.float32), 'We2': lin(ks[4], OUT_DIM, 1), 'be2': jnp.zeros((1,), jnp.float32), 'Wn1': lin(ks[5], OUT_DIM, OUT_DIM), 'bn1': jnp.zeros((OUT_DIM,), jnp.float32), 'Wn2': lin(ks[6], OUT_DIM, 1), 'bn2': jnp.zeros((1,), jnp.float32), 'Wg': lin(ks[7], 2 * OUT_DIM, OUT_DIM), 'bg': jnp.zeros((OUT_DIM,), jnp.float32), 'g2': jnp.ones((OUT_DIM,), jnp.float32), 'bt2': jnp.zeros((OUT_DIM,), jnp.float32)}
    _L0_gnn_all = _L0_gnn_setup()
    _L0_gnn_in = {k: v for k, v in _L0_gnn_all.items() if k in ('W1', 'b1', 'g1', 'bt1', 'We1', 'be1', 'We2', 'be2', 'Wn1', 'bn1', 'Wn2', 'bn2', 'Wg', 'bg', 'g2', 'bt2')}
    del _L0_gnn_all
    return {'x': x, 'src': src, 'dst': dst, 'L0_gnn_W1': _L0_gnn_in['W1'], 'L0_gnn_b1': _L0_gnn_in['b1'], 'L0_gnn_g1': _L0_gnn_in['g1'], 'L0_gnn_bt1': _L0_gnn_in['bt1'], 'L0_gnn_We1': _L0_gnn_in['We1'], 'L0_gnn_be1': _L0_gnn_in['be1'], 'L0_gnn_We2': _L0_gnn_in['We2'], 'L0_gnn_be2': _L0_gnn_in['be2'], 'L0_gnn_Wn1': _L0_gnn_in['Wn1'], 'L0_gnn_bn1': _L0_gnn_in['bn1'], 'L0_gnn_Wn2': _L0_gnn_in['Wn2'], 'L0_gnn_bn2': _L0_gnn_in['bn2'], 'L0_gnn_Wg': _L0_gnn_in['Wg'], 'L0_gnn_bg': _L0_gnn_in['bg'], 'L0_gnn_g2': _L0_gnn_in['g2'], 'L0_gnn_bt2': _L0_gnn_in['bt2']}

def reference(x, src, dst, L0_gnn_W1, L0_gnn_b1, L0_gnn_g1, L0_gnn_bt1, L0_gnn_We1, L0_gnn_be1, L0_gnn_We2, L0_gnn_be2, L0_gnn_Wn1, L0_gnn_bn1, L0_gnn_Wn2, L0_gnn_bn2, L0_gnn_Wg, L0_gnn_bg, L0_gnn_g2, L0_gnn_bt2):
    import jax
    import jax.numpy as jnp

    def _L0_gnn_ref(x, edge_index, W1, b1, g1, bt1, We1, be1, We2, be2, Wn1, bn1, Wn2, bn2, Wg, bg, g2, bt2):
        import jax, jax.numpy as jnp
        import numpy as np
        LN_EPS = 1e-05
        N_NODES = 6250
        IN_DIM = 128
        OUT_DIM = 128
        N_EDGES = 100000

        def _ln(x, g, b):
            m = jnp.mean(x, axis=-1, keepdims=True)
            v = jnp.mean((x - m) ** 2, axis=-1, keepdims=True)
            return (x - m) * jax.lax.rsqrt(v + LN_EPS) * g + b
        n = x.shape[0]
        h = jax.nn.relu(_ln(x @ W1 + b1, g1, bt1))
        row, col = (edge_index[0], edge_index[1])
        h_src = h[row]
        ef = jnp.concatenate([h_src, h[col]], axis=1)
        edge_weights = jax.nn.sigmoid(jax.nn.relu(ef @ We1 + be1) @ We2 + be2)[:, 0]
        node_weights = jax.nn.sigmoid(jax.nn.relu(h @ Wn1 + bn1) @ Wn2 + bn2)[:, 0]
        _ = node_weights
        aggr = jax.ops.segment_sum(edge_weights[:, None] * h_src, col, num_segments=n)
        gate = jax.nn.sigmoid(jnp.concatenate([h, aggr], axis=-1) @ Wg + bg)
        h_new = gate * aggr + (1.0 - gate) * h
        return _ln(h_new, g2, bt2)
    edge_index = jnp.stack([src, dst])
    x = _layernorm(x + _L0_gnn_ref(x, edge_index, L0_gnn_W1, L0_gnn_b1, L0_gnn_g1, L0_gnn_bt1, L0_gnn_We1, L0_gnn_be1, L0_gnn_We2, L0_gnn_be2, L0_gnn_Wn1, L0_gnn_bn1, L0_gnn_Wn2, L0_gnn_bn2, L0_gnn_Wg, L0_gnn_bg, L0_gnn_g2, L0_gnn_bt2), axis=-1)
    return x

_drawn_inputs = setup_inputs


def setup_inputs(seed=0):
    import zlib

    import numpy as np

    out = dict(_drawn_inputs(seed))
    spreads = {'L0_gnn_b1': (0.0, 0.1),
     'L0_gnn_g1': (1.0, 0.2),
     'L0_gnn_bt1': (0.0, 0.1),
     'L0_gnn_be1': (0.0, 0.672),
     'L0_gnn_bn1': (0.0, 0.1),
     'L0_gnn_bg': (0.0, 0.321),
     'L0_gnn_g2': (1.0, 0.2),
     'L0_gnn_bt2': (0.0, 0.1)}
    factors = {}
    for name, (base, spread) in spreads.items():
        noise = np.random.default_rng([zlib.crc32(name.encode()), seed]).standard_normal(out[name].shape)
        drawn = base * np.exp(spread * noise) if base else spread * noise
        out[name] = jnp.asarray(drawn.astype(out[name].dtype))
    for name, factor in factors.items():
        out[name] = (out[name] * factor).astype(out[name].dtype)
    return out
```

```python
import concourse.bass as bass
from concourse import mybir
from contextlib import ExitStack


def gnn_layer(nc, x, src, dst, W1, b1, g1, bt1, We1, be1, We2, be2, Wg, bg, g2, bt2, out):
    f32, bf16, i32, u32 = mybir.dt.float32, mybir.dt.bfloat16, mybir.dt.int32, mybir.dt.uint32
    ALU, ACT, AX = mybir.AluOpType, mybir.ActivationFunctionType, mybir.AxisListType.X
    ds = bass.ds

    P = 128
    EPS = 1e-5
    N, D = x.shape
    E = src.shape[0]
    BLOCKS = -(-N // P)
    LAST = N - (BLOCKS - 1) * P
    STEP = 7
    STEPS = BLOCKS // STEP
    assert D == P and STEPS * STEP == BLOCKS and 96 < LAST < P
    BIG = P * BLOCKS - 1
    W = STEP * D

    TILES = 4
    SLOTS = 8
    HALF = SLOTS // 2
    AHEAD = 4
    GE = TILES * P
    GROUPS = -(-E // (GE * SLOTS)) * SLOTS
    ROUNDS = GROUPS // SLOTS
    RW = 2048
    RT, RG = RW // P, RW // GE
    ROWS = GROUPS * GE // RW
    FULL = E // RW
    REST = E - FULL * RW
    assert ROWS * RW == GROUPS * GE and 96 < ROWS <= P and FULL == ROWS - 1 and REST
    STAGED = HALF * TILES
    EDGE_TILES = GROUPS * TILES

    ctx = ExitStack()
    with ctx:
        def sb(name, shape, dt=f32):
            return ctx.enter_context(nc.sbuf_tensor(name, shape, dt))

        def sem(name):
            return ctx.enter_context(nc.semaphore(name))

        table = nc.dram_tensor("node_table", [BLOCKS * P, 2 * D], f32)

        x_all = sb("x_all", [P, BLOCKS, D])
        h_all = sb("h_all", [P, BLOCKS, D])
        aggr = sb("aggr", [P, BLOCKS, D])
        b_parts = sb("b_parts", [P, BLOCKS, 3, D], bf16)
        src_idx = sb("src_idx", [P, EDGE_TILES + SLOTS * TILES], i32)
        dst_col = sb("dst_col", [P, EDGE_TILES])
        region = sb("region", [P, SLOTS * TILES * 2 * D])
        src_rows = region[0:ROWS, 0:RW].bitcast(i32)
        dst_rows = region[0:ROWS, RW:2 * RW].bitcast(i32)
        src_rows_f = region[0:ROWS, 2 * RW:3 * RW]
        dst_rows_f = region[0:ROWS, 3 * RW:4 * RW]
        a_all = region[:, 0:BLOCKS * D].rearrange("p (b f) -> p b f", f=D)
        ring = region[:, :].rearrange("p (t f) -> p t f", f=2 * D)
        idx_stage = sb("idx_stage", [P, 2, STAGED], i32)
        onehot = sb("onehot", [P, 4 * GE], bf16)
        onehotT = sb("onehotT", [P, 2 * GE], bf16)
        weighted = sb("weighted", [P, GE])
        score = sb("score", [P, 2 * TILES])
        weight = sb("weight", [P, 2 * TILES])
        relu_dot = sb("relu_dot", [P, 2 * GE], bf16)
        tmp = sb("tmp", [P, 2, W])
        gate = sb("gate", [P, W])
        stats = sb("stats", [P, STEP, 6])
        mv = sb("mv", [P, BLOCKS, 2])
        mv_step = sb("mv_step", [P, STEP, 2])
        sd = sb("sd", [P, BLOCKS])
        rstd = sb("rstd", [P, BLOCKS])
        ident = sb("ident", [P, P])
        ident_bf = sb("ident_bf", [P, P], bf16)
        iota_sb = sb("iota_sb", [P, P])
        neg_base = sb("neg_base", [P, BLOCKS])
        eps = sb("eps", [P, 1])
        w1_sb = sb("w1_sb", [P, D])
        we1_sb = sb("we1_sb", [P, 2 * D])
        wg_sb = sb("wg_sb", [P, 2, D])
        b1_bc, g1_bc, bt1_bc, be1_bc, we2_bc, bg_bc, g2_bc, bt2_bc = (
            sb(n, [P, D]) for n in ("b1_bc", "g1_bc", "bt1_bc", "be1_bc", "we2_bc", "bg_bc", "g2_bc", "bt2_bc"))
        be2_bc = sb("be2_bc", [P, 1])
        bounds = sb("bounds", [P, RG, 2], i32)
        extremes = sb("extremes", [P, RG, 2])
        group_bounds = sb("group_bounds", [1, GROUPS * 2], i32)
        spans = sb("spans", [1, GROUPS])
        zeros = sb("zeros", [1, GROUPS])
        visit_ends_f = sb("visit_ends_f", [1, GROUPS])
        visit_ends = sb("visit_ends", [1, AHEAD + GROUPS], i32)

        psum = ctx.enter_context(nc.psum_tensor("psum", [P, 4096], f32))
        ps_x = psum[:, 0:W]
        ps_h = psum[:, 1024:1024 + W]
        ps_a = psum[:, 2048:2048 + W]
        ps_b = psum[:, 3072:3072 + W]
        BANK = 512
        ps_onehotT = psum[:, 0:2 * BANK].bitcast(bf16)
        ps_z = psum[:, 2 * BANK:4 * BANK]
        ps_sum = psum[:, 4 * BANK:6 * BANK]
        iota = psum[:, 6 * BANK:6 * BANK + P]

        x_in = [sem(f"x_in{i}") for i in range(STEPS)]
        x_ready = sem("x_ready")
        src_loaded = sem("src_loaded")
        dst_loaded = sem("dst_loaded")
        params_in = sem("params_in")
        pads_set = sem("pads_set")
        consts_zeroed = sem("consts_zeroed")
        consts_set = sem("consts_set")
        ident_bf_set = sem("ident_bf_set")
        src_cast = sem("src_cast")
        dst_cast = sem("dst_cast")
        cols_T = sem("cols_T")
        cols_out = sem("cols_out")
        extremes_set = sem("extremes_set")
        bounds_cast = sem("bounds_cast")
        bounds_set = sem("bounds_set")
        bounds_moved = sem("bounds_moved")
        ends_set = sem("ends_set")
        xT_psum = sem("xT_psum")
        xT_set = sem("xT_set")
        pre_psum = sem("pre_psum")
        pre_set = sem("pre_set")
        stats_set = sem("stats_set")
        mv_set = sem("mv_set")
        aggregated = sem("aggregated")
        dve_turn = sem("dve_turn")
        sd_set = sem("sd_set")
        rstd_set = sem("rstd_set")
        centred = sem("centred")
        normed = sem("normed")
        h_set = sem("h_set")
        hT_psum = sem("hT_psum")
        hT_set = sem("hT_set")
        ab_psum = sem("ab_psum")
        a_set = sem("a_set")
        b_set = sem("b_set")
        table_stored = sem("table_stored")
        hi_set = sem("hi_set")
        rest1_set = sem("rest1_set")
        mid_set = sem("mid_set")
        lo_set = sem("lo_set")
        edge_ready = sem("edge_ready")
        edges_done = sem("edges_done")
        xb_set = sem("xb_set")
        idx_staged = [sem(f"idx_staged{i}") for i in range(2)]
        gathered = [sem(f"gathered{i}") for i in range(SLOTS)]
        groups_ready = sem("groups_ready")
        slots_free = sem("slots_free")
        pool_turn = sem("pool_turn")
        onehot_set = sem("onehot_set")
        onehotT_psum = sem("onehotT_psum")
        onehotT_set = sem("onehotT_set")
        z_psum = sem("z_psum")
        score_set = sem("score_set")
        weight_set = sem("weight_set")
        weighted_set = sem("weighted_set")
        sum_psum = sem("sum_psum")
        aggr_set = sem("aggr_set")
        hgT_psum = sem("hgT_psum")
        hgT_set = sem("hgT_set")
        gate_psum = sem("gate_psum")
        gate_in = sem("gate_in")
        gate_set = sem("gate_set")
        diff_set = sem("diff_set")
        gated = sem("gated")
        mixed = sem("mixed")
        mv2_set = sem("mv2_set")
        sd2_set = sem("sd2_set")
        rstd2_set = sem("rstd2_set")
        centred2 = sem("centred2")
        y_set = sem("y_set")
        mv3_set = sem("mv3_set")
        sd3_set = sem("sd3_set")
        rstd3_set = sem("rstd3_set")
        out_set = sem("out_set")
        stored = sem("stored")

        LEAD = 3
        FIRST = 2
        PARAMS = 12

        def steps(t, i):
            return t[:, ds(i * STEP, STEP)]

        def step_bc(v):
            return v[:, :].unsqueeze(1).to_broadcast([P, STEP, D])

        def grid(t):
            return t.rearrange("p (b f) -> p b f", f=D)

        def group_blocks(eng, g):
            first = eng.value_load(group_bounds[0:1, ds(g * 2, 1)], min_val=0, max_val=BLOCKS - 1)
            past = eng.value_load(group_bounds[0:1, ds(g * 2 + 1, 1)], min_val=1, max_val=BLOCKS)
            return first, past

        block = ctx.enter_context(nc.Block())

        @block.sync
        def _(sp):
            x_blocks = x[0:(BLOCKS - 1) * P, :].rearrange("(b p) f -> p b f", p=P)
            for i in range(STEPS):
                n = STEP if i < STEPS - 1 else STEP - 1
                sp.dma_start(x_all[:, i * STEP:i * STEP + n, :],
                             x_blocks[:, i * STEP:i * STEP + n, :]).then_inc(x_in[i], 16)
            sp.wait_ge(pads_set, 3)
            sp.dma_start(x_all[0:LAST, BLOCKS - 1, :], x[(BLOCKS - 1) * P:N, :]).then_inc(x_in[STEPS - 1], 16)
            for i in range(STEPS):
                sp.wait_ge(x_in[i], 16 if i < STEPS - 1 else 32)
                sp.sem_inc(x_ready, 1)
            sp.wait_ge(bounds_set, 1)
            sp.dma_start(group_bounds[0:1, :], bounds[0:ROWS, :, :].rearrange("p g b -> p (g b)")).then_inc(bounds_moved, 16)
            tab = table[:, :].rearrange("(b p) f -> p b f", p=P)
            with sp.Fori(0, STEPS) as i:
                sp.wait_ge(h_set, i + 1)
                sp.dma_start(steps(tab, i)[:, :, D:2 * D], steps(h_all, i)).then_inc(table_stored, 16)
                sp.wait_ge(a_set, i + 1)
                sp.dma_start(steps(tab, i)[:, :, 0:D], steps(a_all, i)).then_inc(table_stored, 16)

            sp.wait_ge(cols_out, 8)
            sp.wait_ge(ends_set, 1)
            for half in range(2):
                sp.dma_start(idx_stage[:, half, :], src_idx[:, half * STAGED:(half + 1) * STAGED]).then_inc(idx_staged[half], 16)
            sp.sem_inc(slots_free, AHEAD)
            with sp.Fori(0, ROUNDS) as r:
                for k in range(SLOTS):
                    sp.wait_ge(gathered[k], (r + 1) * (16 * TILES))
                    sp.sem_inc(groups_ready, 1)
                    if k % HALF == HALF - 1:
                        half = k // HALF
                        sp.dma_start(idx_stage[:, half, :],
                                     src_idx[:, ds((r + 1) * (SLOTS * TILES) + half * STAGED, STAGED)]).then_inc(idx_staged[half], 16)
                    end = sp.value_load(visit_ends[0:1, ds(r * SLOTS + k, 1)], min_val=1, max_val=GROUPS * BLOCKS + LEAD)
                    sp.wait_ge(sum_psum, end)
                    sp.sem_inc(slots_free, 1)
            for half in range(2):
                sp.wait_ge(idx_staged[half], 16 * (ROUNDS + 1))

            out_blocks = out[0:(BLOCKS - 1) * P, :].rearrange("(b p) f -> p b f", p=P)
            with sp.Fori(0, STEPS - 1) as i:
                sp.wait_ge(out_set, i + 1)
                sp.dma_start(steps(out_blocks, i), steps(aggr, i)).then_inc(stored, 16)
            sp.wait_ge(out_set, STEPS)
            sp.dma_start(out_blocks[:, (STEPS - 1) * STEP:BLOCKS - 1, :], aggr[:, (STEPS - 1) * STEP:BLOCKS - 1, :]).then_inc(stored, 16)
            sp.dma_start(out[(BLOCKS - 1) * P:N, :], aggr[0:LAST, BLOCKS - 1, :]).then_inc(stored, 16)
            sp.wait_ge(stored, 16 * (STEPS + 1))

        @block.gpsimd
        def _(pool):
            pool.memset(src_idx[:, EDGE_TILES:], 0).then_inc(consts_set, 1)
            pool.memset(ident[:, :], 0.0).then_inc(consts_zeroed, 1)
            pool.memset(eps[:, :], EPS).then_inc(consts_set, 1)
            pool.iota(iota_sb[:, :], pattern=[[1, P]], base=0, channel_multiplier=0,
                      allow_small_or_imprecise_dtypes=True).then_inc(consts_set, 1)
            pool.iota(neg_base[:, :], pattern=[[-P, BLOCKS]], base=0, channel_multiplier=0,
                      allow_small_or_imprecise_dtypes=True).then_inc(consts_set, 1)
            pool.wait_ge(consts_zeroed, 1)
            pool.affine_select(out=ident[:, :], in_=ident[:, :], compare_op=ALU.not_equal, fill=1.0,
                               base=0, pattern=[[-1, P]], channel_multiplier=1).then_inc(consts_set, 1)
            pool.wait_ge(src_loaded, 32)
            pool.tensor_copy(src_rows_f, src_rows).then_inc(src_cast, 1)

            pool.wait_ge(params_in, 16 * PARAMS)
            pool.wait_ge(xT_psum, STEPS)
            with pool.Fori(0, STEPS) as i:
                pool.tensor_tensor(steps(x_all, i), steps(x_all, i), step_bc(bt2_bc), ALU.add).then_inc(xb_set, 1)

            pool.wait_ge(table_stored, 32 * STEPS)
            with pool.Fori(0, ROUNDS) as r:
                for k in range(SLOTS):
                    half, c = k // HALF, (k % HALF) * TILES
                    if k % HALF == 0:
                        pool.wait_ge(idx_staged[half], (r + 1) * 16)
                    pool.wait_ge(slots_free, r * SLOTS + (k + 1))
                    pool.sem_inc(pool_turn, 1)
                    for t in range(TILES):
                        pool.indirect_dma_start(
                            out=ring[:, k * TILES + t, :], out_offset=None, in_=table[:, :],
                            in_offset=bass.IndirectOffsetOnAxis(ap=idx_stage[:, half, c + t:c + t + 1].bitcast(u32), axis=0),
                        ).then_inc(gathered[k], 16)

            pool.wait_ge(edges_done, 1)
            with pool.Fori(0, STEPS) as i:
                pool.wait_ge(hgT_psum, i + 1)
                pool.tensor_tensor(steps(aggr, i), steps(aggr, i), steps(h_all, i), ALU.subtract).then_inc(diff_set, 1)

        @block.scalar
        def _(act):
            act.wait_ge(pads_set, 2)
            for rows, edges, loaded in ((dst_rows, dst, dst_loaded), (src_rows, src, src_loaded)):
                act.dma_start(rows[0:FULL, :], edges[0:FULL * RW].rearrange("(p e) -> p e", e=RW)).then_inc(loaded, 16)
                act.dma_start(rows[FULL:ROWS, 0:REST], edges[FULL * RW:E].rearrange("(p e) -> p e", p=1)).then_inc(loaded, 16)
            act.dma_start(w1_sb[:, :], W1[:, :]).then_inc(params_in, 16)
            act.dma_start(we1_sb[:, :].rearrange("k (c f) -> k c f", c=2), We1.rearrange("(c k) f -> k c f", c=2)).then_inc(params_in, 16)
            act.dma_start(wg_sb[:, :, :], Wg.rearrange("(c k) f -> k c f", c=2)).then_inc(params_in, 16)
            for dst_bc, v in ((b1_bc, b1), (g1_bc, g1), (bt1_bc, bt1), (be1_bc, be1), (we2_bc, We2.rearrange("f o -> (f o)")),
                              (bg_bc, bg), (g2_bc, g2), (bt2_bc, bt2), (be2_bc, be2)):
                n = v.shape[0]
                act.dma_start(dst_bc[:, :], v.rearrange("(o f) -> o f", o=1).to_broadcast([P, n])).then_inc(params_in, 16)

            act.wait_ge(consts_set, 5)
            act.activation(ident_bf[:, :], ident[:, :], ACT.Copy).then_inc(ident_bf_set, 1)
            act.wait_ge(dst_loaded, 32)
            act.activation(dst_rows_f, dst_rows, ACT.Copy).then_inc(dst_cast, 1)
            for n in range(8):
                rows, q = n // 4, n % 4
                act.wait_ge(cols_T, n + 1)
                ps = psum[:, 512 * n:512 * n + 4 * ROWS].rearrange("q (j p) -> q j p", j=4)
                col = (dst_col[:, :] if rows == 0 else src_idx[:, 0:EDGE_TILES]).rearrange("q (p j) -> q j p", j=RT)
                act.activation(col[:, 4 * q:4 * q + 4, :], ps, ACT.Copy).then_inc(cols_out, 1)

            with act.Fori(0, STEPS) as i:
                act.wait_ge(xT_psum, i + 1)
                act.activation(tmp[:, 0, :], ps_x, ACT.Copy).then_inc(xT_set, 1)
            act.wait_ge(mv_set, STEPS)
            act.activation(sd[:, :], mv[:, :, 1], ACT.Sqrt, bias=eps[:, 0:1]).then_inc(sd_set, 1)

            def relu_h(i, n):
                act.wait_ge(normed, n)
                act.activation(steps(h_all, i), steps(h_all, i), ACT.Relu).then_inc(h_set, 1)

            def hT_out(i, n):
                act.wait_ge(hT_psum, n)
                act.activation(tmp[:, 1, :], ps_x, ACT.Copy).then_inc(hT_set, 1)

            def a_out(i, n):
                act.wait_ge(ab_psum, n)
                act.activation(steps(a_all, i), grid(ps_a), ACT.Copy).then_inc(a_set, 1)

            relu_h(0, 1)
            hT_out(0, 1)
            with act.Fori(0, STEPS - 1) as i:
                relu_h(i + 1, i + 2)
                a_out(i, i + 1)
                hT_out(i + 1, i + 2)
            a_out(STEPS - 1, STEPS)

            with act.Fori(0, STEPS) as i:
                act.wait_ge(b_set, i + 1)
                act.activation(steps(b_parts, i)[:, :, 0, :], steps(aggr, i), ACT.Copy).then_inc(hi_set, 1)
                act.wait_ge(rest1_set, i + 1)
                act.activation(steps(b_parts, i)[:, :, 1, :], steps(aggr, i), ACT.Copy).then_inc(mid_set, 1)

            act.sem_inc(onehotT_set, FIRST - 1 + LEAD)
            act.sem_inc(weight_set, FIRST - 2 + LEAD)
            act.sem_inc(weighted_set, FIRST - 2 + LEAD)
            act.wait_ge(bounds_moved, 16)
            act.wait_ge(edge_ready, 1)
            visit = act.alloc_register("act_visit")
            act.reg_mov(visit, FIRST)

            def weigh(v):
                act.wait_ge(score_set, v + LEAD)
                half = act.snap((v % 2) * TILES)
                act.activation(weight[:, ds(half, TILES)], score[:, ds(half, TILES)], ACT.Sigmoid, bias=be2_bc[:, 0:1]).then_inc(weight_set, 1)
                act.wait_ge(weight_set, v + LEAD)
                act.wait_ge(sum_psum, v - 1 + LEAD)
                for t in range(TILES):
                    last = act.activation(weighted[:, t * P:(t + 1) * P], onehot[:, ds((v % 4) * GE + t * P, P)],
                                          ACT.Copy, scale=weight[:, ds(half + t, 1)])
                last.then_inc(weighted_set, 1)

            with act.Fori(0, GROUPS) as g:
                first, past = group_blocks(act, g)
                with act.Fori(first, past) as b:
                    v = act.snap(visit, min_val=FIRST, max_val=FIRST + GROUPS * BLOCKS)
                    act.wait_ge(onehotT_psum, v + LEAD)
                    act.wait_ge(z_psum, v - 2 + LEAD)
                    act.activation(onehotT[:, ds((v % 2) * GE, GE)], ps_onehotT[:, ds((v % 2) * 2 * BANK, GE)], ACT.Copy).then_inc(onehotT_set, 1)
                    weigh(v - 1)
                    act.reg_add(visit, visit, 1)
            v = act.snap(visit, min_val=FIRST, max_val=FIRST + GROUPS * BLOCKS)
            weigh(v - 1)

            def transposes_out(i):
                act.wait_ge(hgT_psum, i + 1)
                act.activation(tmp[:, 0, :], ps_x, ACT.Copy)
                act.activation(tmp[:, 1, :], ps_h, ACT.Copy).then_inc(hgT_set, 1)

            def sigmoid_gate(i):
                act.wait_ge(gate_in, i + 1)
                act.activation(gate[:, :], ps_a, ACT.Sigmoid).then_inc(gate_set, 1)

            transposes_out(0)
            act.wait_ge(gate_psum, 1)
            transposes_out(1)
            sigmoid_gate(0)
            with act.Fori(1, STEPS - 1) as i:
                act.wait_ge(gate_psum, i + 1)
                transposes_out(i + 1)
                act.wait_ge(gated, i)
                sigmoid_gate(i)
            act.wait_ge(gated, STEPS - 1)
            sigmoid_gate(STEPS - 1)
            act.wait_ge(mv2_set, STEPS)
            act.activation(sd[:, :], mv[:, :, 1], ACT.Sqrt, bias=eps[:, 0:1]).then_inc(sd2_set, 1)
            act.wait_ge(mv3_set, STEPS)
            act.activation(sd[:, :], mv[:, :, 1], ACT.Sqrt, bias=eps[:, 0:1]).then_inc(sd3_set, 1)

        @block.tensor
        def _(pe):
            pe.wait_ge(consts_set, 5)
            pe.wait_ge(ident_bf_set, 1)
            for n in range(8):
                pe.wait_ge(dst_cast if n < 4 else src_cast, 1)
                rows = dst_rows_f if n < 4 else src_rows_f
                for j in range(4):
                    c = (4 * (n % 4) + j) * P
                    last = pe.transpose(psum[:, BANK * n + j * ROWS:BANK * n + (j + 1) * ROWS], rows[:, c:c + P], ident[0:ROWS, 0:ROWS])
                last.then_inc(cols_T, 1)

            def transpose_x(i, n):
                pe.wait_ge(x_ready, n)
                if n != 1:
                    pe.wait_ge(xT_set, n - 1)
                for t in range(STEP):
                    last = pe.transpose(ps_x[:, t * P:(t + 1) * P], x_all[:, i * STEP + t, :], ident[:, :])
                last.then_inc(xT_psum, 1)

            def product_x(i, n):
                pe.wait_ge(xT_set, n)
                if n != 1:
                    pe.wait_ge(pre_set, n - 1)
                for t in range(STEP):
                    last = pe.matmul(ps_h[:, t * P:(t + 1) * P], tmp[:, 0, t * P:(t + 1) * P], w1_sb[:, :], start=True, stop=True)
                last.then_inc(pre_psum, 1)

            pe.wait_ge(cols_out, 8)
            pe.wait_ge(params_in, 16 * PARAMS)
            for i in range(STEPS):
                transpose_x(i, i + 1)
                product_x(i, i + 1)

            def transpose_h(i, n):
                pe.wait_ge(h_set, n)
                if n != 1:
                    pe.wait_ge(hT_set, n - 1)
                for t in range(STEP):
                    last = pe.transpose(ps_x[:, t * P:(t + 1) * P], h_all[:, i * STEP + t, :], ident[:, :])
                last.then_inc(hT_psum, 1)

            def product_h(i, n):
                pe.wait_ge(hT_set, n)
                if n != 1:
                    pe.wait_ge(a_set, n - 1)
                    pe.wait_ge(b_set, n - 1)
                for t in range(STEP):
                    for c, ps in enumerate((ps_a, ps_b)):
                        last = pe.matmul(ps[:, t * D:(t + 1) * D], tmp[:, 1, t * P:(t + 1) * P], we1_sb[:, c * D:(c + 1) * D], start=True, stop=True)
                last.then_inc(ab_psum, 1)

            transpose_h(0, 1)
            for i in range(STEPS):
                if i + 1 < STEPS:
                    transpose_h(i + 1, i + 2)
                product_h(i, i + 1)

            pe.sem_inc(onehotT_psum, FIRST - 1 + LEAD)
            pe.sem_inc(z_psum, FIRST - 1 + LEAD)
            pe.sem_inc(sum_psum, FIRST - 3 + LEAD)
            pe.wait_ge(bounds_moved, 16)
            pe.wait_ge(edge_ready, 1)
            visit, slot_1, slot_2 = (pe.alloc_register(f"pe_{n}") for n in ("visit", "slot_1", "slot_2"))
            pe.reg_mov(visit, FIRST)
            pe.reg_mov(slot_1, 0)
            pe.reg_mov(slot_2, 0)

            def held(slot_reg):
                return pe.snap(slot_reg, min_val=0, max_val=SLOTS - 1)

            def sum_rows(v, slot):
                pe.wait_ge(weighted_set, v + LEAD)
                pe.wait_ge(aggr_set, v - 2 + LEAD)
                for t in range(TILES):
                    last = pe.matmul(ps_sum[:, ds((v % 2) * BANK, D)], weighted[:, t * P:(t + 1) * P],
                                     region[:, ds(slot * (TILES * 2 * D) + (t * 2 * D + D), D)], start=(t == 0), stop=(t == TILES - 1))
                last.then_inc(sum_psum, 1)

            with pe.Fori(0, GROUPS) as g:
                first, past = group_blocks(pe, g)
                slot = pe.snap(g % SLOTS, min_val=0, max_val=SLOTS - 1)
                with pe.Fori(first, past) as b:
                    v = pe.snap(visit, min_val=FIRST, max_val=FIRST + GROUPS * BLOCKS)
                    pe.wait_ge(onehot_set, v + LEAD)
                    pe.wait_ge(onehotT_set, v - 2 + LEAD)
                    for t in range(TILES):
                        last = pe.transpose(ps_onehotT[:, ds((v % 2) * 2 * BANK + t * P, P)], onehot[:, ds((v % 4) * GE + t * P, P)], ident_bf[:, :])
                    last.then_inc(onehotT_psum, 1)
                    before = held(slot_2)
                    pe.wait_ge(groups_ready, g + 1)
                    sum_rows(v - 2, before)
                    pe.wait_ge(score_set, v - 2 + LEAD)
                    pe.matmul(ps_z[:, ds((v % 2) * BANK, GE)].rearrange("p (t f) -> p t f", f=D), ident[:, :], ring[:, ds(slot * TILES, TILES), 0:D], start=True, stop=False)
                    pe.wait_ge(onehotT_set, v + LEAD)
                    for t in range(TILES):
                        for k in range(3):
                            last = pe.matmul(ps_z[:, ds((v % 2) * BANK + t * D, D)], onehotT[:, ds((v % 2) * GE + t * P, P)],
                                             b_parts[:, ds(b, 1), k, :], start=False, stop=(t == TILES - 1 and k == 2))
                    last.then_inc(z_psum, 1)
                    pe.reg_mov(slot_2, slot_1)
                    pe.reg_mov(slot_1, slot)
                    pe.reg_add(visit, visit, 1)
            v = pe.snap(visit, min_val=FIRST, max_val=FIRST + GROUPS * BLOCKS)
            before_2, before_1 = held(slot_2), held(slot_1)
            sum_rows(v - 2, before_2)
            sum_rows(v - 1, before_1)

            pe.wait_ge(edges_done, 1)

            def transpose_both(i, n):
                if n != 1:
                    pe.wait_ge(hgT_set, n - 1)
                for ps, t_all in ((ps_x, aggr), (ps_h, h_all)):
                    for t in range(STEP):
                        last = pe.transpose(ps[:, t * P:(t + 1) * P], t_all[:, i * STEP + t, :], ident[:, :])
                last.then_inc(hgT_psum, 1)

            def gate_product(i, n):
                pe.wait_ge(hgT_set, n)
                if n != 1:
                    pe.wait_ge(gate_set, n - 1)
                for t in range(STEP):
                    pe.matmul(ps_a[:, t * D:(t + 1) * D], tmp[:, 1, t * P:(t + 1) * P], wg_sb[:, 0, :], start=True, stop=False)
                    last = pe.matmul(ps_a[:, t * D:(t + 1) * D], tmp[:, 0, t * P:(t + 1) * P], wg_sb[:, 1, :], start=False, stop=True)
                last.then_inc(gate_psum, 1)

            transpose_both(0, 1)
            for i in range(STEPS):
                if i + 1 < STEPS:
                    transpose_both(i + 1, i + 2)
                gate_product(i, i + 1)

        @block.vector
        def _(dve):
            dve.memset(src_rows[96:ROWS, :], 0).then_inc(pads_set, 1)
            dve.memset(dst_rows[96:ROWS, :], BIG).then_inc(pads_set, 1)
            dve.memset(x_all[96:P, BLOCKS - 1, :], 0.0).then_inc(pads_set, 1)
            dve.memset(zeros[:, :], 0.0)
            dve.memset(onehot[:, :], 0.0)
            dve.memset(weighted[:, :], 0.0)
            dve.memset(visit_ends[:, 0:AHEAD], 1)
            dve.wait_ge(dst_loaded, 32)
            ext = extremes[0:ROWS, :, :]
            by_group = dst_rows.rearrange("p (g e) -> p g e", e=GE)
            dve.tensor_reduce(ext[:, :, 0], by_group, AX, ALU.min)
            dve.tensor_reduce(ext[:, :, 1], by_group, AX, ALU.max).then_inc(extremes_set, 1)
            dve.wait_ge(extremes_set, 1)
            dve.tensor_copy(bounds[0:ROWS, :, 0], ext[:, :, 0])
            dve.tensor_scalar(bounds[0:ROWS, :, 1], ext[:, :, 1], float(P), None, ALU.add).then_inc(bounds_cast, 1)
            dve.wait_ge(bounds_cast, 1)
            dve.tensor_scalar(bounds[0:ROWS, :, :], bounds[0:ROWS, :, :], 7, None, ALU.arith_shift_right).then_inc(bounds_set, 1)

            def statistics(t, i, done, n, prior):
                dve.sem_inc(dve_turn, 1)
                for c in range(STEP):
                    last = dve.bn_stats(stats[:, c, :], t[:, ds(i * STEP + c, 1), :])
                last.then_inc(stats_set, 1)
                dve.wait_ge(stats_set, prior + n)
                dve.sem_inc(dve_turn, 1)
                for c in range(STEP):
                    last = dve.bn_aggr(mv_step[:, c, :], stats[:, c, :])
                last.then_inc(aggregated, 1)
                dve.wait_ge(aggregated, prior + n)
                dve.tensor_copy(steps(mv, i), mv_step[:, :, :]).then_inc(done, 1)

            dve.wait_ge(params_in, 16 * PARAMS)
            with dve.Fori(0, STEPS) as i:
                dve.wait_ge(pre_psum, i + 1)
                dve.tensor_tensor(steps(h_all, i), grid(ps_h), step_bc(b1_bc), ALU.add).then_inc(pre_set, 1)
                dve.wait_ge(pre_set, i + 1)
                statistics(h_all, i, mv_set, i + 1, 0)

            dve.wait_ge(bounds_moved, 16)
            both = group_bounds[0:1, :].rearrange("p (g b) -> p g b", b=2)
            dve.tensor_tensor(spans[:, :], both[:, :, 1], both[:, :, 0], ALU.subtract).then_inc(bounds_cast, 1)
            dve.wait_ge(bounds_cast, 2)
            dve.tensor_tensor_scan(visit_ends_f[:, :], spans[:, :], zeros[:, :], float(FIRST - 1 + LEAD), ALU.add, ALU.add).then_inc(bounds_cast, 1)
            dve.wait_ge(bounds_cast, 3)
            dve.tensor_copy(visit_ends[:, AHEAD:], visit_ends_f[:, :]).then_inc(ends_set, 1)

            dve.wait_ge(sd_set, 1)
            dve.reciprocal(rstd[:, :], sd[:, :]).then_inc(rstd_set, 1)
            dve.wait_ge(rstd_set, 1)

            def normalise(t, i, scale_bc, shift, centred_n, done):
                for c in range(STEP):
                    b = i * STEP + c
                    last = dve.scalar_tensor_tensor(t[:, ds(b, 1), :], t[:, ds(b, 1), :], mv[:, ds(b, 1), 0], scale_bc[:, :].unsqueeze(1),
                                                    ALU.subtract, ALU.mult)
                last.then_inc(centred, 1)
                dve.wait_ge(centred, centred_n)
                for c in range(STEP):
                    b = i * STEP + c
                    last = dve.scalar_tensor_tensor(t[:, ds(b, 1), :], t[:, ds(b, 1), :], rstd[:, ds(b, 1)], shift(b), ALU.mult, ALU.add)
                last.then_inc(done, 1)

            def norm_h(i, n):
                normalise(h_all, i, g1_bc, lambda b: bt1_bc[:, :].unsqueeze(1), n, normed)

            def b_out(i, n):
                dve.wait_ge(ab_psum, n)
                dve.tensor_tensor(steps(aggr, i), grid(ps_b), step_bc(be1_bc), ALU.add).then_inc(b_set, 1)

            norm_h(0, 1)
            with dve.Fori(0, STEPS - 1) as i:
                norm_h(i + 1, i + 2)
                b_out(i, i + 1)
            b_out(STEPS - 1, STEPS)

            with dve.Fori(0, STEPS) as i:
                dve.wait_ge(hi_set, i + 1)
                dve.tensor_tensor(steps(aggr, i), steps(aggr, i), steps(b_parts, i)[:, :, 0, :], ALU.subtract).then_inc(rest1_set, 1)
                dve.wait_ge(mid_set, i + 1)
                dve.tensor_tensor(steps(b_parts, i)[:, :, 2, :], steps(aggr, i), steps(b_parts, i)[:, :, 1, :], ALU.subtract).then_inc(lo_set, 1)

            dve.wait_ge(lo_set, STEPS)
            dve.wait_ge(a_set, STEPS)
            dve.memset(aggr[:, :, :], 0.0)
            dve.memset(ps_z[:, BANK:2 * BANK], 0.0)
            dve.wait_ge(consts_set, 5)
            dve.tensor_copy(iota, iota_sb[:, :]).then_inc(edge_ready, 1)
            dve.wait_ge(edge_ready, 1)
            dve.wait_ge(cols_out, 8)
            dve.sem_inc(onehot_set, FIRST - 1 + LEAD)
            dve.sem_inc(score_set, FIRST - 2 + LEAD)
            dve.sem_inc(aggr_set, FIRST - 3 + LEAD)
            visit, block_1, block_2 = (dve.alloc_register(f"dve_{n}") for n in ("visit", "block_1", "block_2"))
            dve.reg_mov(visit, FIRST)
            dve.reg_mov(block_1, 0)
            dve.reg_mov(block_2, 0)

            def score_edges(v):
                dve.wait_ge(z_psum, v + LEAD)
                for t in range(TILES):
                    last = dve.scalar_tensor_tensor(relu_dot[:, ds((v % 2) * GE + t * D, D)], ps_z[:, ds((v % 2) * BANK + t * D, D)], 0.0, we2_bc[:, :], ALU.max, ALU.mult,
                                                    accum_out=score[:, ds((v % 2) * TILES + t, 1)])
                last.then_inc(score_set, 1)

            def add_sums(v, block_reg):
                b = dve.snap(block_reg, min_val=0, max_val=BLOCKS - 1)
                dve.wait_ge(sum_psum, v + LEAD)
                dve.wait_ge(aggr_set, v - 1 + LEAD)
                own = aggr[:, :, :].rearrange("p b f -> p (b f)")[:, ds(b * D, D)]
                dve.tensor_tensor(own, own, ps_sum[:, ds((v % 2) * BANK, D)], ALU.add).then_inc(aggr_set, 1)

            with dve.Fori(0, GROUPS) as g:
                first, past = group_blocks(dve, g)
                with dve.Fori(first, past) as b:
                    v = dve.snap(visit, min_val=FIRST, max_val=FIRST + GROUPS * BLOCKS)
                    dve.wait_ge(weighted_set, v - 4 + LEAD)
                    for t in range(TILES):
                        last = dve.tensor_scalar(onehot[:, ds((v % 4) * GE + t * P, P)], iota, dst_col[:, ds(g * TILES + t, 1)], neg_base[:, ds(b, 1)],
                                                 ALU.subtract, ALU.is_equal)
                    last.then_inc(onehot_set, 1)
                    score_edges(v - 1)
                    add_sums(v - 2, block_2)
                    dve.reg_mov(block_2, block_1)
                    dve.reg_mov(block_1, b)
                    dve.reg_add(visit, visit, 1)
            v = dve.snap(visit, min_val=FIRST, max_val=FIRST + GROUPS * BLOCKS)
            score_edges(v - 1)
            add_sums(v - 2, block_2)
            add_sums(v - 1, block_1)
            dve.wait_ge(aggr_set, v - 1 + LEAD)
            dve.sem_inc(edges_done, 1)

            def bias_gate(i, n):
                dve.wait_ge(gate_psum, n)
                dve.tensor_tensor(grid(ps_a), grid(ps_a), step_bc(bg_bc), ALU.add).then_inc(gate_in, 1)

            def mix(i, n):
                dve.wait_ge(diff_set, n)
                dve.wait_ge(gate_set, n)
                dve.tensor_tensor(steps(aggr, i), steps(aggr, i), grid(gate[:, :]), ALU.mult).then_inc(gated, 1)
                dve.wait_ge(gated, n)
                dve.tensor_tensor(steps(aggr, i), steps(aggr, i), steps(h_all, i), ALU.add).then_inc(mixed, 1)
                dve.wait_ge(mixed, n)
                statistics(aggr, i, mv2_set, n, STEPS)

            bias_gate(0, 1)
            with dve.Fori(0, STEPS - 1) as i:
                mix(i, i + 1)
                bias_gate(i + 1, i + 2)
            mix(STEPS - 1, STEPS)

            dve.wait_ge(sd2_set, 1)
            dve.reciprocal(rstd[:, :], sd[:, :]).then_inc(rstd_set, 1)
            dve.wait_ge(rstd_set, 2)
            dve.wait_ge(xb_set, STEPS)
            with dve.Fori(0, STEPS) as i:
                normalise(aggr, i, g2_bc, lambda b: x_all[:, ds(b, 1), :], i + (STEPS + 1), y_set)
            dve.wait_ge(y_set, STEPS)
            with dve.Fori(0, STEPS) as i:
                statistics(aggr, i, mv3_set, i + 1, 2 * STEPS)
            dve.wait_ge(sd3_set, 1)
            dve.reciprocal(rstd[:, :], sd[:, :]).then_inc(rstd_set, 1)
            dve.wait_ge(rstd_set, 3)
            with dve.Fori(0, STEPS) as i:
                for c in range(STEP):
                    b = i * STEP + c
                    last = dve.tensor_scalar(aggr[:, ds(b, 1), :], aggr[:, ds(b, 1), :], mv[:, ds(b, 1), 0], rstd[:, ds(b, 1)],
                                             ALU.subtract, ALU.mult)
                last.then_inc(out_set, 1)


_INS = ["x", "src", "dst", "L0_gnn_W1", "L0_gnn_b1", "L0_gnn_g1", "L0_gnn_bt1", "L0_gnn_We1", "L0_gnn_be1", "L0_gnn_We2",
        "L0_gnn_be2", "L0_gnn_Wg", "L0_gnn_bg", "L0_gnn_g2", "L0_gnn_bt2"]


def kernel(**inputs):
    import numpy as _np
    import concourse.bacc as _bacc
    from concourse import mybir as _mybir
    from concourse.bass_utils import run_bass_kernel_spmd as _run

    nc = _bacc.Bacc("TRN2", target_bir_lowering=False, num_devices=1)
    arrays, args = {}, []
    for name in _INS:
        a = _np.ascontiguousarray(inputs[name])
        arrays[f"in_{name}_dram"] = a
        args.append(nc.dram_tensor(f"in_{name}_dram", a.shape, _mybir.dt.from_np(a.dtype), kind="ExternalInput").ap())
    args.append(nc.dram_tensor("out_0_dram", arrays["in_x_dram"].shape, _mybir.dt.float32, kind="ExternalOutput").ap())
    gnn_layer(nc, *args)
    r = _run(nc, [arrays], core_ids=[0])
    return r.results[0]["out_0_dram"]
```

```python
import concourse.bass as bass
from concourse import mybir
from contextlib import ExitStack


def gnn_layer(nc, x, src, dst, W1, b1, g1, bt1, We1, be1, We2, be2, Wg, bg, g2, bt2, out):
    f32, bf16, i32, u32 = mybir.dt.float32, mybir.dt.bfloat16, mybir.dt.int32, mybir.dt.uint32
    ALU, ACT, AX = mybir.AluOpType, mybir.ActivationFunctionType, mybir.AxisListType.X
    ds = bass.ds

    P = 128
    EPS = 1e-5
    N, D = x.shape
    E = src.shape[0]
    BLOCKS = -(-N // P)
    LAST = N - (BLOCKS - 1) * P
    STEP = 7
    STEPS = BLOCKS // STEP
    assert D == P and STEPS * STEP == BLOCKS and 96 < LAST < P
    BIG = P * BLOCKS - 1
    W = STEP * D

    TILES = 4
    SLOTS = 8
    HALF = SLOTS // 2
    AHEAD = 4
    GE = TILES * P
    GROUPS = -(-E // (GE * SLOTS)) * SLOTS
    ROUNDS = GROUPS // SLOTS
    RW = 2048
    RT, RG = RW // P, RW // GE
    ROWS = GROUPS * GE // RW
    FULL = E // RW
    REST = E - FULL * RW
    assert ROWS * RW == GROUPS * GE and 96 < ROWS <= P and FULL == ROWS - 1 and REST
    STAGED = HALF * TILES
    EDGE_TILES = GROUPS * TILES
    WINDOWS = 4
    B_AHEAD = 3
    LAG = 2
    NODES = (BLOCKS + 2) * P

    ctx = ExitStack()
    with ctx:
        def sb(name, shape, dt=f32):
            return ctx.enter_context(nc.sbuf_tensor(name, shape, dt))

        def sem(name):
            return ctx.enter_context(nc.semaphore(name))

        table = nc.dram_tensor("node_table", [BLOCKS * P, 2 * D], f32)
        b_table = nc.dram_tensor("b_table", [NODES, 3 * D], bf16)
        first_dram = nc.dram_tensor("first_dram", [1, GROUPS], f32)

        x_all = sb("x_all", [P, BLOCKS, D])
        h_all = sb("h_all", [P, BLOCKS, D])
        hT_all = sb("hT_all", [P, BLOCKS * P])
        aggrT = sb("aggrT", [P, NODES])
        a_all = aggrT[:, 0:BLOCKS * D].rearrange("p (b f) -> p b f", f=D)
        src_idx = sb("src_idx", [P, EDGE_TILES + SLOTS * TILES], i32)
        dst_in = sb("dst_in", [P, EDGE_TILES])
        region = sb("region", [P, SLOTS * TILES * 2 * D])
        src_rows = region[0:ROWS, 0:RW].bitcast(i32)
        dst_rows = region[0:ROWS, RW:2 * RW].bitcast(i32)
        src_rows_f = region[0:ROWS, 2 * RW:3 * RW]
        dst_rows_f = region[0:ROWS, 3 * RW:4 * RW]
        ring = region[:, :].rearrange("p (t f) -> p t f", f=2 * D)
        idx_stage = sb("idx_stage", [P, 2, STAGED], i32)
        b_window = sb("b_window", [P, WINDOWS, 3, D], bf16)
        onehot = sb("onehot", [P, 4, TILES, P], bf16)
        onehotT = sb("onehotT", [P, 2, TILES, P], bf16)
        weighted = sb("weighted", [P, 2, TILES, P])
        score = sb("score", [P, 2, TILES])
        weight = sb("weight", [P, 2, TILES])
        relu_dot = sb("relu_dot", [P, 2, TILES, D], bf16)
        shifted = sb("shifted", [P, TILES])
        tmp = sb("tmp", [P, W])
        b_f = sb("b_f", [P, 2, W])
        b_parts = sb("b_parts", [P, 2, STEP, 3, D], bf16)
        gate = sb("gate", [P, W])
        stats = sb("stats", [P, 2, STEP, 6])
        mv = sb("mv", [P, BLOCKS, 2])
        sd = sb("sd", [P, BLOCKS])
        rstd = sb("rstd", [P, BLOCKS])
        ident = sb("ident", [P, P])
        ident_bf = sb("ident_bf", [P, P], bf16)
        iota_sb = sb("iota_sb", [P, P])
        shifts = sb("shifts", [P, BLOCKS + 1])
        eps = sb("eps", [P, 1])
        w1_sb = sb("w1_sb", [P, D])
        we1_sb = sb("we1_sb", [P, 2 * D])
        wg_sb = sb("wg_sb", [P, 2, D])
        b1_bc, g1_bc, bt1_bc, be1_bc, we2_bc, bg_bc, g2_bc, bt2_bc = (
            sb(n, [P, D]) for n in ("b1_bc", "g1_bc", "bt1_bc", "be1_bc", "we2_bc", "bg_bc", "g2_bc", "bt2_bc"))
        be2_bc = sb("be2_bc", [P, 1])
        least = sb("least", [P, RG])
        greatest = sb("greatest", [P, RG])
        first_int = sb("first_int", [P, RG], i32)
        span_int = sb("span_int", [P, RG], i32)
        first_row = sb("first_row", [1, LAG + GROUPS + B_AHEAD], i32)
        more_row = sb("more_row", [1, GROUPS], i32)
        most_more = sb("most_more", [1, 1], i32)
        last_window = sb("last_window", [1, GROUPS], i32)
        first_bc = sb("first_bc", [P, GROUPS])

        psum = ctx.enter_context(nc.psum_tensor("psum", [P, 4096], f32))
        ps_x = psum[:, 0:W]
        ps_h = psum[:, 1024:1024 + W]
        ps_a = psum[:, 2048:2048 + W]
        ps_b = psum[:, 3072:3072 + W]
        BANK = 512
        ps_onehotT = [psum[:, i * BANK:(i + 1) * BANK].bitcast(bf16)[:, 0:GE].rearrange("p (t n) -> p t n", n=P) for i in range(2)]
        ps_z = [psum[:, (2 + i) * BANK:(3 + i) * BANK].rearrange("p (t f) -> p t f", f=D) for i in range(2)]
        ps_sum = [psum[:, (4 + i) * BANK:(4 + i) * BANK + P] for i in range(2)]
        iota = psum[:, 6 * BANK:6 * BANK + P]

        x_in = [sem(f"x_in{i}") for i in range(STEPS)]
        x_ready = sem("x_ready")
        src_loaded = sem("src_loaded")
        dst_loaded = sem("dst_loaded")
        params_in = sem("params_in")
        pads_set = sem("pads_set")
        consts_zeroed = sem("consts_zeroed")
        consts_set = sem("consts_set")
        ident_bf_set = sem("ident_bf_set")
        src_cast = sem("src_cast")
        dst_cast = sem("dst_cast")
        cols_T = sem("cols_T")
        cols_out = sem("cols_out")
        extremes_set = sem("extremes_set")
        first_set = sem("first_set")
        span_set = sem("span_set")
        rows_in = sem("rows_in")
        bc_moved = sem("bc_moved")
        bc_in = sem("bc_in")
        more_set = sem("more_set")
        local_set = sem("local_set")
        xT_psum = sem("xT_psum")
        xT_set = sem("xT_set")
        pre_psum = sem("pre_psum")
        pre_set = sem("pre_set")
        stats_set = sem("stats_set")
        mv_set = sem("mv_set")
        sd_set = sem("sd_set")
        rstd_set = sem("rstd_set")
        centred = sem("centred")
        normed = sem("normed")
        h_set = sem("h_set")
        hT_psum = sem("hT_psum")
        hT_set = sem("hT_set")
        a_psum = sem("a_psum")
        b_psum = sem("b_psum")
        a_set = sem("a_set")
        b_set = sem("b_set")
        table_stored = sem("table_stored")
        hi_set = sem("hi_set")
        rest1_set = sem("rest1_set")
        mid_set = sem("mid_set")
        lo_set = sem("lo_set")
        edge_ready = sem("edge_ready")
        edges_done = sem("edges_done")
        all_done = sem("all_done")
        b_padded = sem("b_padded")
        b_stored = [sem(f"b_stored{i}") for i in range(2)]
        aggr_psum = sem("aggr_psum")
        first_params_in = sem("first_params_in")
        xb_set = sem("xb_set")
        idx_staged = [sem(f"idx_staged{i}") for i in range(2)]
        gathered = [sem(f"gathered{i}") for i in range(SLOTS)]
        b_loaded = [sem(f"b_loaded{i}") for i in range(WINDOWS)]
        groups_ready = sem("groups_ready")
        slots_free = sem("slots_free")
        pool_turn = sem("pool_turn")
        onehot_set = sem("onehot_set")
        onehotT_psum = sem("onehotT_psum")
        onehotT_set = sem("onehotT_set")
        z_psum = sem("z_psum")
        z_added = sem("z_added")
        score_set = sem("score_set")
        weight_set = sem("weight_set")
        weighted_set = sem("weighted_set")
        sum_psum = sem("sum_psum")
        aggr_set = sem("aggr_set")
        more = {n: sem("more_" + n) for n in ("staged", "gathered", "b_loaded", "shifted", "onehot", "onehotT_psum", "onehotT",
                                              "z_psum", "z_added", "score", "weight", "weighted", "sum_psum", "aggr")}
        gate_psum = sem("gate_psum")
        gate_in = sem("gate_in")
        gate_set = sem("gate_set")
        diff_set = sem("diff_set")
        gated = sem("gated")
        mixed = sem("mixed")
        mv2_set = sem("mv2_set")
        sd2_set = sem("sd2_set")
        y_set = sem("y_set")
        mv3_set = sem("mv3_set")
        sd3_set = sem("sd3_set")
        out_set = sem("out_set")
        stored = sem("stored")

        LEAD = 5
        PARAMS = 10

        def steps(t, i):
            return t[:, ds(i * STEP, STEP)]

        def step_bc(v):
            return v[:, :].unsqueeze(1).to_broadcast([P, STEP, D])

        def grid(t):
            return t.rearrange("p (b f) -> p b f", f=D)

        def ring_a(slot):
            return ring[:, slot * TILES:(slot + 1) * TILES, 0:D]

        def counts(eng, r):
            held = {k: eng.snap(r * SLOTS + (k + LEAD), min_val=1, max_val=GROUPS + LEAD) for k in range(-4, SLOTS)}
            return held.__getitem__

        def spread_onehot(eng, g_local, out_onehot):
            return eng.tensor_tensor(out_onehot, iota.unsqueeze(1).to_broadcast([P, TILES, P]),
                                     g_local.unsqueeze(2).to_broadcast([P, TILES, P]), ALU.is_equal)

        def transpose_onehot(eng, i_onehot, i):
            for t in range(TILES):
                last = eng.transpose(ps_onehotT[i][:, t, :], onehot[:, i_onehot, t, :], ident_bf[:, :])
            return last

        def spread_b(eng, i, window):
            for t in range(TILES):
                for k in range(3):
                    last = eng.matmul(ps_z[i][:, t, :], onehotT[:, i, t, :], b_window[:, window, k, :], start=(k == 0), stop=(k == 2))
            return last

        def add_a(eng, i, slot):
            return eng.tensor_tensor(ps_z[i], ps_z[i], ring_a(slot), ALU.add)

        def score_edges(eng, i):
            for t in range(TILES):
                last = eng.scalar_tensor_tensor(relu_dot[:, i, t, :], ps_z[i][:, t, :], 0.0, we2_bc[:, :], ALU.max, ALU.mult,
                                                accum_out=score[:, i, t:t + 1])
            return last

        def sigmoid_score(eng, i):
            return eng.activation(weight[:, i, :], score[:, i, :], ACT.Sigmoid, bias=be2_bc[:, 0:1])

        def weigh(eng, i, i_onehot):
            for t in range(TILES):
                last = eng.activation(weighted[:, i, t, :], onehot[:, i_onehot, t, :], ACT.Copy, scale=weight[:, i, t:t + 1])
            return last

        def sum_rows(eng, i, slot):
            for t in range(TILES):
                last = eng.matmul(ps_sum[i], ring[:, slot * TILES + t, D:2 * D], weighted[:, i, t, :], start=(t == 0), stop=(t == TILES - 1))
            return last

        def add_sums(eng, i, first):
            return eng.tensor_tensor(aggrT[:, ds(first, P)], aggrT[:, ds(first, P)], ps_sum[i], ALU.add)

        block = ctx.enter_context(nc.Block())

        @block.sync
        def _(sp):
            x_blocks = x[0:(BLOCKS - 1) * P, :].rearrange("(b p) f -> p b f", p=P)
            for i in range(STEPS):
                n = STEP if i < STEPS - 1 else STEP - 1
                sp.dma_start(x_all[:, i * STEP:i * STEP + n, :],
                             x_blocks[:, i * STEP:i * STEP + n, :]).then_inc(x_in[i], 16)
            sp.wait_ge(pads_set, 5)
            sp.dma_start(x_all[0:LAST, BLOCKS - 1, :], x[(BLOCKS - 1) * P:N, :]).then_inc(x_in[STEPS - 1], 16)
            for i in range(STEPS):
                sp.wait_ge(x_in[i], 16 if i < STEPS - 1 else 32)
                sp.sem_inc(x_ready, 1)
            sp.wait_ge(first_set, 2)
            sp.dma_start(first_row[0:1, LAG:LAG + GROUPS], first_int[0:ROWS, :]).then_inc(rows_in, 16)
            sp.dma_start(first_dram[0:1, :].rearrange("o (p g) -> (o p) g", g=RG), least[0:ROWS, :]).then_inc(bc_moved, 16)
            sp.wait_ge(span_set, 1)
            sp.dma_start(more_row[0:1, :], span_int[0:ROWS, :]).then_inc(rows_in, 16)
            sp.wait_ge(bc_moved, 16)
            sp.dma_start(first_bc[:, :], first_dram[0:1, :].to_broadcast([P, GROUPS])).then_inc(bc_in, 16)
            tab = table[:, :].rearrange("(b p) f -> p b f", p=P)
            with sp.Fori(0, STEPS) as i:
                sp.wait_ge(h_set, i + 1)
                sp.dma_start(steps(tab, i)[:, :, D:2 * D], steps(h_all, i)).then_inc(table_stored, 16)
                sp.wait_ge(a_set, i + 1)
                sp.dma_start(steps(tab, i)[:, :, 0:D], steps(a_all, i)).then_inc(table_stored, 16)
            sp.wait_ge(cols_out, 8)
            for half in range(2):
                sp.dma_start(idx_stage[:, half, :], src_idx[:, half * STAGED:(half + 1) * STAGED]).then_inc(idx_staged[half], 16)
            sp.sem_inc(slots_free, AHEAD)
            for i in range(2):
                sp.dma_start(b_table[(BLOCKS + i) * P:(BLOCKS + i + 1) * P, :].rearrange("p (k f) -> p k f", k=3), onehot[:, i, 0:3, :]).then_inc(b_padded, 16)
            b_tab = b_table[0:BLOCKS * P, :].rearrange("(b p) (k f) -> p b k f", p=P, k=3)
            for i in range(STEPS):
                sp.wait_ge(lo_set, i + 1)
                sp.dma_start(b_tab[:, i * STEP:(i + 1) * STEP], b_parts[:, i % 2]).then_inc(b_stored[i % 2], 16)

            def load_window(group, window):
                first = sp.value_load(first_row[0:1, ds(group + LAG, 1)], min_val=0, max_val=BIG)
                sp.dma_start(b_window[:, window, :, :], b_table[ds(first, P), :].rearrange("p (k f) -> p k f", k=3)).then_inc(b_loaded[window], 16)

            sp.wait_ge(rows_in, 32)
            sp.wait_ge(b_padded, 32)
            for i in range(2):
                sp.wait_ge(b_stored[i], 16 * ((STEPS + 1 - i) // 2))
            sp.sem_inc(groups_ready, LEAD - 1)
            for g in range(B_AHEAD):
                load_window(g, g)
            with sp.Fori(0, ROUNDS) as r:
                at = counts(sp, r)
                for k in range(SLOTS):
                    sp.wait_ge(gathered[k], (r + 1) * (16 * TILES))
                    sp.sem_inc(groups_ready, 1)
                    if k % HALF == HALF - 1:
                        half = k // HALF
                        sp.dma_start(idx_stage[:, half, :],
                                     src_idx[:, ds((r + 1) * (SLOTS * TILES) + half * STAGED, STAGED)]).then_inc(idx_staged[half], 16)
                    sp.wait_ge(sum_psum, at(k - AHEAD))
                    sp.sem_inc(slots_free, 1)
                    sp.wait_ge(z_psum, at(k - 1))
                    load_window(r * SLOTS + (k + B_AHEAD), (k + B_AHEAD) % WINDOWS)
            for half in range(2):
                sp.wait_ge(idx_staged[half], 16 * (ROUNDS + 1))
            for j in range(WINDOWS):
                sp.wait_ge(b_loaded[j], 16 * (GROUPS // WINDOWS + (j < B_AHEAD)))

            sp.wait_ge(more_set, 1)
            any_more = sp.value_load(most_more[0:1, 0:1], min_val=0, max_val=BLOCKS)
            with sp.If(any_more > 0):
                sp.wait_ge(edges_done, 1)
                done = sp.alloc_register("sp_done")
                sp.reg_mov(done, 1)
                sp.sem_inc(more["aggr"], 1)
                with sp.Fori(0, GROUPS) as g:
                    n = sp.snap(done, min_val=1, max_val=GROUPS * BLOCKS)
                    sp.wait_ge(more["aggr"], n)
                    sp.dma_start(idx_stage[:, 0, 0:TILES], src_idx[:, ds(g * TILES, TILES)]).then_inc(more["staged"], 16)
                    first = sp.value_load(first_row[0:1, ds(g + LAG, 1)], min_val=0, max_val=BIG)
                    last = sp.value_load(last_window[0:1, ds(g, 1)], min_val=2, max_val=BLOCKS)
                    with sp.Fori(1, last) as w:
                        n = sp.snap(done, min_val=1, max_val=GROUPS * BLOCKS)
                        sp.wait_ge(more["aggr"], n)
                        at_node = sp.snap((first + w * P).with_bounds(min_val=0, max_val=BIG + P))
                        sp.dma_start(b_window[:, 0, :, :], b_table[ds(at_node, P), :].rearrange("p (k f) -> p k f", k=3)).then_inc(more["b_loaded"], 16)
                        sp.reg_add(done, done, 1)

            out_blocks = out[0:(BLOCKS - 1) * P, :].rearrange("(b p) f -> p b f", p=P)
            with sp.Fori(0, STEPS - 1) as i:
                sp.wait_ge(out_set, i + 1)
                sp.dma_start(steps(out_blocks, i), steps(h_all, i)).then_inc(stored, 16)
            sp.wait_ge(out_set, STEPS)
            sp.dma_start(out_blocks[:, (STEPS - 1) * STEP:BLOCKS - 1, :], h_all[:, (STEPS - 1) * STEP:BLOCKS - 1, :]).then_inc(stored, 16)
            sp.dma_start(out[(BLOCKS - 1) * P:N, :], h_all[0:LAST, BLOCKS - 1, :]).then_inc(stored, 16)
            sp.wait_ge(stored, 16 * (STEPS + 1))

        @block.gpsimd
        def _(pool):
            pool.memset(src_idx[:, EDGE_TILES:], 0).then_inc(consts_set, 1)
            pool.memset(ident[:, :], 0.0).then_inc(consts_zeroed, 1)
            pool.memset(eps[:, :], EPS).then_inc(consts_set, 1)
            pool.iota(iota_sb[:, :], pattern=[[1, P]], base=0, channel_multiplier=0,
                      allow_small_or_imprecise_dtypes=True).then_inc(consts_set, 1)
            pool.iota(shifts[:, :], pattern=[[P, BLOCKS + 1]], base=0, channel_multiplier=0,
                      allow_small_or_imprecise_dtypes=True).then_inc(consts_set, 1)
            pool.wait_ge(consts_zeroed, 1)
            pool.affine_select(out=ident[:, :], in_=ident[:, :], compare_op=ALU.not_equal, fill=1.0,
                               base=0, pattern=[[-1, P]], channel_multiplier=1).then_inc(consts_set, 1)
            pool.wait_ge(src_loaded, 32)
            pool.tensor_copy(src_rows_f, src_rows).then_inc(src_cast, 1)

            pool.wait_ge(params_in, 16 * PARAMS)
            pool.wait_ge(xT_psum, STEPS)
            with pool.Fori(0, STEPS) as i:
                pool.tensor_tensor(steps(x_all, i), steps(x_all, i), step_bc(bt2_bc), ALU.add).then_inc(xb_set, 1)

            pool.wait_ge(table_stored, 32 * STEPS)
            with pool.Fori(0, ROUNDS) as r:
                for k in range(SLOTS):
                    half, c = k // HALF, (k % HALF) * TILES
                    if k % HALF == 0:
                        pool.wait_ge(idx_staged[half], (r + 1) * 16)
                    pool.wait_ge(slots_free, r * SLOTS + (k + 1))
                    pool.sem_inc(pool_turn, 1)
                    for t in range(TILES):
                        pool.indirect_dma_start(
                            out=ring[:, k * TILES + t, :], out_offset=None, in_=table[:, :],
                            in_offset=bass.IndirectOffsetOnAxis(ap=idx_stage[:, half, c + t:c + t + 1].bitcast(u32), axis=0),
                        ).then_inc(gathered[k], 16)

            pool.wait_ge(more_set, 1)
            any_more = pool.value_load(most_more[0:1, 0:1], min_val=0, max_val=BLOCKS)
            with pool.If(any_more > 0):
                with pool.Fori(0, GROUPS) as g:
                    pool.wait_ge(more["staged"], (g + 1) * 16)
                    pool.sem_inc(pool_turn, 1)
                    for t in range(TILES):
                        pool.indirect_dma_start(
                            out=ring[:, t, :], out_offset=None, in_=table[:, :],
                            in_offset=bass.IndirectOffsetOnAxis(ap=idx_stage[:, 0, t:t + 1].bitcast(u32), axis=0),
                        ).then_inc(more["gathered"], 16)

        @block.scalar
        def _(act):
            act.dma_start(w1_sb[:, :], W1[:, :]).then_inc(first_params_in, 16)
            act.dma_start(b1_bc[:, :], b1.rearrange("(o f) -> o f", o=1).to_broadcast([P, D])).then_inc(first_params_in, 16)
            act.wait_ge(pads_set, 2)
            for rows, edges, loaded in ((dst_rows, dst, dst_loaded), (src_rows, src, src_loaded)):
                act.dma_start(rows[0:FULL, :], edges[0:FULL * RW].rearrange("(p e) -> p e", e=RW)).then_inc(loaded, 16)
                act.dma_start(rows[FULL:ROWS, 0:REST], edges[FULL * RW:E].rearrange("(p e) -> p e", p=1)).then_inc(loaded, 16)
            for dst_bc, v in ((g1_bc, g1), (bt1_bc, bt1), (be1_bc, be1), (we2_bc, We2.rearrange("f o -> (f o)")),
                              (bg_bc, bg), (g2_bc, g2), (bt2_bc, bt2), (be2_bc, be2)):
                n = v.shape[0]
                act.dma_start(dst_bc[:, :], v.rearrange("(o f) -> o f", o=1).to_broadcast([P, n])).then_inc(params_in, 16)
            act.dma_start(we1_sb[:, :].rearrange("k (c f) -> k c f", c=2), We1.rearrange("(c k) f -> k c f", c=2)).then_inc(params_in, 16)
            act.dma_start(wg_sb[:, :, :], Wg.rearrange("(c k) f -> k c f", c=2)).then_inc(params_in, 16)

            act.preload_act_table(ACT.Sqrt)
            act.wait_ge(consts_set, 5)
            act.activation(ident_bf[:, :], ident[:, :], ACT.Copy).then_inc(ident_bf_set, 1)
            act.wait_ge(dst_loaded, 32)
            act.activation(dst_rows_f, dst_rows, ACT.Copy).then_inc(dst_cast, 1)
            for n in range(8):
                rows, q = n // 4, n % 4
                act.wait_ge(cols_T, n + 1)
                ps = psum[:, 512 * n:512 * n + 4 * ROWS].rearrange("q (j p) -> q j p", j=4)
                col = (dst_in[:, :] if rows == 0 else src_idx[:, 0:EDGE_TILES]).rearrange("q (p j) -> q j p", j=RT)
                act.activation(col[:, 4 * q:4 * q + 4, :], ps, ACT.Copy).then_inc(cols_out, 1)

            with act.Fori(0, STEPS) as i:
                act.wait_ge(xT_psum, i + 1)
                act.activation(tmp[:, :], ps_x, ACT.Copy).then_inc(xT_set, 1)
            act.wait_ge(mv_set, STEPS)
            act.activation(sd[:, :], mv[:, :, 1], ACT.Sqrt, bias=eps[:, 0:1]).then_inc(sd_set, 1)

            def relu_h(i, n):
                act.wait_ge(normed, n)
                act.activation(steps(h_all, i), steps(h_all, i), ACT.Relu).then_inc(h_set, 1)

            def hT_out(i, n):
                act.wait_ge(hT_psum, n)
                act.activation(hT_all[:, ds(i * W, W)], ps_x, ACT.Copy).then_inc(hT_set, 1)

            def a_out(i, n):
                act.wait_ge(a_psum, n)
                act.activation(steps(a_all, i), grid(ps_a), ACT.Copy).then_inc(a_set, 1)

            relu_h(0, 1)
            hT_out(0, 1)
            with act.Fori(0, STEPS - 1) as i:
                relu_h(i + 1, i + 2)
                a_out(i, i + 1)
                hT_out(i + 1, i + 2)
            a_out(STEPS - 1, STEPS)

            for i in range(STEPS):
                b_step = grid(b_f[:, i % 2, :])
                act.wait_ge(b_set, i + 1)
                if i >= 2:
                    act.wait_ge(b_stored[i % 2], 16 * (i // 2))
                act.activation(b_parts[:, i % 2, :, 0, :], b_step, ACT.Copy).then_inc(hi_set, 1)
                act.wait_ge(rest1_set, i + 1)
                act.activation(b_parts[:, i % 2, :, 1, :], b_step, ACT.Copy).then_inc(mid_set, 1)

            act.preload_act_table(ACT.Sigmoid)
            act.sem_inc(onehotT_set, LEAD - 1)
            act.sem_inc(weight_set, LEAD - 2)
            act.sem_inc(weighted_set, LEAD - 2)

            def weigh_group(at, k):
                act.wait_ge(score_set, at(k))
                sigmoid_score(act, k % 2).then_inc(weight_set, 1)
                act.wait_ge(weight_set, at(k))
                act.wait_ge(sum_psum, at(k - 2))
                weigh(act, k % 2, k % 4).then_inc(weighted_set, 1)

            with act.Fori(0, ROUNDS) as r:
                at = counts(act, r)
                for k in range(SLOTS):
                    act.wait_ge(onehotT_psum, at(k))
                    act.wait_ge(z_psum, at(k - 2))
                    act.activation(onehotT[:, k % 2], ps_onehotT[k % 2], ACT.Copy).then_inc(onehotT_set, 1)
                    weigh_group(at, k - 1)
            weigh_group(lambda k: GROUPS + k + LEAD, -1)

            act.wait_ge(more_set, 1)
            any_more = act.value_load(most_more[0:1, 0:1], min_val=0, max_val=BLOCKS)
            with act.If(any_more > 0):
                done = act.alloc_register("act_done")
                act.reg_mov(done, 1)
                with act.Fori(0, GROUPS) as g:
                    last = act.value_load(last_window[0:1, ds(g, 1)], min_val=2, max_val=BLOCKS)
                    with act.Fori(1, last) as w:
                        n = act.snap(done, min_val=1, max_val=GROUPS * BLOCKS)
                        act.wait_ge(more["onehotT_psum"], n)
                        act.activation(onehotT[:, 0], ps_onehotT[0], ACT.Copy).then_inc(more["onehotT"], 1)
                        act.wait_ge(more["score"], n)
                        sigmoid_score(act, 0).then_inc(more["weight"], 1)
                        act.wait_ge(more["weight"], n)
                        weigh(act, 0, 0).then_inc(more["weighted"], 1)
                        act.reg_add(done, done, 1)

            for i in range(STEPS):
                act.wait_ge(gate_in, i + 1)
                if i:
                    act.wait_ge(gated, i)
                act.activation(gate[:, :], ps_a, ACT.Sigmoid).then_inc(gate_set, 1)
            act.wait_ge(mv2_set, STEPS)
            act.activation(sd[:, :], mv[:, :, 1], ACT.Sqrt, bias=eps[:, 0:1]).then_inc(sd2_set, 1)
            act.wait_ge(mv3_set, STEPS)
            act.activation(sd[:, :], mv[:, :, 1], ACT.Sqrt, bias=eps[:, 0:1]).then_inc(sd3_set, 1)

        @block.tensor
        def _(pe):
            pe.wait_ge(consts_set, 5)
            pe.wait_ge(ident_bf_set, 1)
            for n in range(8):
                pe.wait_ge(dst_cast if n < 4 else src_cast, 1)
                rows = dst_rows_f if n < 4 else src_rows_f
                for j in range(4):
                    c = (4 * (n % 4) + j) * P
                    last = pe.transpose(psum[:, BANK * n + j * ROWS:BANK * n + (j + 1) * ROWS], rows[:, c:c + P], ident[0:ROWS, 0:ROWS])
                last.then_inc(cols_T, 1)

            def transpose_x(i, n):
                pe.wait_ge(x_ready, n)
                if n != 1:
                    pe.wait_ge(xT_set, n - 1)
                for t in range(STEP):
                    last = pe.transpose(ps_x[:, t * P:(t + 1) * P], x_all[:, i * STEP + t, :], ident[:, :])
                last.then_inc(xT_psum, 1)

            def product_x(i, n):
                pe.wait_ge(xT_set, n)
                if n != 1:
                    pe.wait_ge(pre_set, n - 1)
                for t in range(STEP):
                    last = pe.matmul(ps_h[:, t * P:(t + 1) * P], tmp[:, t * P:(t + 1) * P], w1_sb[:, :], start=True, stop=True)
                last.then_inc(pre_psum, 1)

            pe.wait_ge(cols_out, 8)
            pe.wait_ge(first_params_in, 32)
            for i in range(STEPS):
                transpose_x(i, i + 1)
                product_x(i, i + 1)

            def transpose_h(i, n):
                pe.wait_ge(h_set, n)
                if n != 1:
                    pe.wait_ge(hT_set, n - 1)
                for t in range(STEP):
                    last = pe.transpose(ps_x[:, t * P:(t + 1) * P], h_all[:, i * STEP + t, :], ident[:, :])
                last.then_inc(hT_psum, 1)

            def product_h(i, ps, half):
                for t in range(i * STEP, (i + 1) * STEP):
                    c = t - i * STEP
                    last = pe.matmul(ps[:, c * D:(c + 1) * D], hT_all[:, t * P:(t + 1) * P], we1_sb[:, half * D:(half + 1) * D], start=True, stop=True)
                return last

            pe.wait_ge(params_in, 16 * PARAMS)
            transpose_h(0, 1)
            for i in range(STEPS):
                if i + 1 < STEPS:
                    transpose_h(i + 1, i + 2)
                pe.wait_ge(hT_set, i + 1)
                if i:
                    pe.wait_ge(a_set, i)
                product_h(i, ps_a, 0).then_inc(a_psum, 1)
            for i in range(STEPS):
                if i:
                    pe.wait_ge(b_set, i)
                product_h(i, ps_b, 1).then_inc(b_psum, 1)

            pe.sem_inc(onehotT_psum, LEAD - 1)
            pe.sem_inc(z_psum, LEAD - 1)
            pe.sem_inc(sum_psum, LEAD - 3)
            pe.wait_ge(edge_ready, 1)

            def sum_group(at, k):
                pe.wait_ge(weighted_set, at(k))
                pe.wait_ge(aggr_set, at(k - 2))
                sum_rows(pe, k % 2, k % SLOTS).then_inc(sum_psum, 1)

            with pe.Fori(0, ROUNDS) as r:
                at = counts(pe, r)
                loaded = [pe.snap((r * 2 + j + 1) * 16, min_val=16, max_val=32 * ROUNDS) for j in range(2)]
                for k in range(SLOTS):
                    pe.wait_ge(onehot_set, at(k))
                    pe.wait_ge(onehotT_set, at(k - 2))
                    transpose_onehot(pe, k % 4, k % 2).then_inc(onehotT_psum, 1)
                    sum_group(at, k - 2)
                    pe.wait_ge(score_set, at(k - 2))
                    pe.wait_ge(b_loaded[k % WINDOWS], loaded[k // WINDOWS])
                    pe.wait_ge(onehotT_set, at(k))
                    spread_b(pe, k % 2, k % WINDOWS).then_inc(z_psum, 1)
            for k in (-2, -1):
                sum_group(lambda k: GROUPS + k + LEAD, k)

            pe.wait_ge(more_set, 1)
            any_more = pe.value_load(most_more[0:1, 0:1], min_val=0, max_val=BLOCKS)
            with pe.If(any_more > 0):
                done = pe.alloc_register("pe_done")
                pe.reg_mov(done, 1)
                with pe.Fori(0, GROUPS) as g:
                    last = pe.value_load(last_window[0:1, ds(g, 1)], min_val=2, max_val=BLOCKS)
                    with pe.Fori(1, last) as w:
                        n = pe.snap(done, min_val=1, max_val=GROUPS * BLOCKS)
                        pe.wait_ge(more["onehot"], n)
                        transpose_onehot(pe, 0, 0).then_inc(more["onehotT_psum"], 1)
                        pe.wait_ge(more["onehotT"], n)
                        pe.wait_ge(more["b_loaded"], n * 16)
                        spread_b(pe, 0, 0).then_inc(more["z_psum"], 1)
                        pe.wait_ge(more["weighted"], n)
                        sum_rows(pe, 0, 0).then_inc(more["sum_psum"], 1)
                        pe.reg_add(done, done, 1)

            pe.wait_ge(all_done, 1)
            for i in range(STEPS):
                if i:
                    pe.wait_ge(diff_set, i)
                for t in range(STEP):
                    b = i * STEP + t
                    last = pe.transpose(ps_x[:, t * P:(t + 1) * P], aggrT[:, b * P:(b + 1) * P], ident[:, :])
                last.then_inc(aggr_psum, 1)
                if i:
                    pe.wait_ge(gate_set, i)
                for t in range(STEP):
                    b = i * STEP + t
                    pe.matmul(ps_a[:, t * D:(t + 1) * D], hT_all[:, b * P:(b + 1) * P], wg_sb[:, 0, :], start=True, stop=False)
                    last = pe.matmul(ps_a[:, t * D:(t + 1) * D], aggrT[:, b * P:(b + 1) * P], wg_sb[:, 1, :], start=False, stop=True)
                last.then_inc(gate_psum, 1)

        @block.vector
        def _(dve):
            dve.memset(src_rows[96:ROWS, :], 0).then_inc(pads_set, 1)
            dve.memset(dst_rows[96:ROWS, :], BIG).then_inc(pads_set, 1)
            dve.memset(x_all[96:P, BLOCKS - 1, :], 0.0).then_inc(pads_set, 1)
            dve.memset(onehot[:, :, :, :], 0.0).then_inc(pads_set, 1)
            dve.memset(weighted[:, :, :, :], 0.0)
            dve.memset(first_row[:, :], 0).then_inc(pads_set, 1)
            dve.wait_ge(dst_loaded, 32)
            by_group = dst_rows.rearrange("p (g e) -> p g e", e=GE)
            dve.tensor_reduce(least[0:ROWS, :], by_group, AX, ALU.min).then_inc(first_set, 1)
            dve.tensor_reduce(greatest[0:ROWS, :], by_group, AX, ALU.max).then_inc(extremes_set, 1)
            dve.wait_ge(extremes_set, 1)
            dve.tensor_copy(first_int[0:ROWS, :], least[0:ROWS, :]).then_inc(first_set, 1)
            dve.tensor_tensor(span_int[0:ROWS, :], greatest[0:ROWS, :], least[0:ROWS, :], ALU.subtract).then_inc(span_set, 1)

            def statistics(t, i, done, n):
                for c in range(STEP):
                    last = dve.bn_stats(stats[:, n % 2, c, :], t[:, i * STEP + c, :])
                last.then_inc(stats_set, 1)
                dve.wait_ge(stats_set, n + 1)
                for c in range(STEP):
                    last = dve.bn_aggr(mv[:, i * STEP + c, :], stats[:, n % 2, c, :])
                last.then_inc(done, 1)

            def normalise(t, i, scale_bc, shift, n, done):
                blocks = range(i * STEP, (i + 1) * STEP)
                for b in blocks:
                    last = dve.scalar_tensor_tensor(t[:, b, :], t[:, b, :], mv[:, b, 0:1], scale_bc[:, :], ALU.subtract, ALU.mult)
                last.then_inc(centred, 1)
                dve.wait_ge(centred, n)
                for b in blocks:
                    last = dve.scalar_tensor_tensor(t[:, b, :], t[:, b, :], rstd[:, b:b + 1], shift(b), ALU.mult, ALU.add)
                last.then_inc(done, 1)

            def at_step(t, i):
                return t[:, i * STEP:(i + 1) * STEP]

            dve.wait_ge(first_params_in, 32)
            for i in range(STEPS):
                dve.wait_ge(pre_psum, i + 1)
                dve.tensor_tensor(at_step(h_all, i), grid(ps_h), step_bc(b1_bc), ALU.add).then_inc(pre_set, 1)
                dve.wait_ge(pre_set, i + 1)
                statistics(h_all, i, mv_set, i)

            dve.wait_ge(params_in, 16 * PARAMS)
            dve.wait_ge(sd_set, 1)
            dve.reciprocal(rstd[:, :], sd[:, :]).then_inc(rstd_set, 1)
            dve.wait_ge(rstd_set, 1)
            for i in range(STEPS):
                normalise(h_all, i, g1_bc, lambda b: bt1_bc[:, :], i + 1, normed)

            dve.wait_ge(cols_out, 8)
            dve.wait_ge(bc_in, 16)
            by_tile = dst_in[:, :].rearrange("p (g t) -> p g t", t=TILES)
            dve.tensor_tensor(by_tile, by_tile, first_bc[:, :].unsqueeze(2).to_broadcast([P, GROUPS, TILES]), ALU.subtract).then_inc(local_set, 1)
            dve.wait_ge(rows_in, 32)
            dve.tensor_scalar(more_row[:, :], more_row[:, :], 7, None, ALU.arith_shift_right).then_inc(local_set, 1)
            dve.wait_ge(local_set, 2)
            dve.tensor_reduce(most_more[:, :], more_row[:, :], AX, ALU.max)
            dve.tensor_scalar(last_window[:, :], more_row[:, :], 1.0, 1.0, ALU.max, ALU.add).then_inc(more_set, 1)

            def b_out(i):
                dve.wait_ge(b_psum, i + 1)
                dve.tensor_tensor(grid(b_f[:, i % 2, :]), grid(ps_b), step_bc(be1_bc), ALU.add).then_inc(b_set, 1)

            b_out(0)
            for i in range(STEPS):
                b_step = grid(b_f[:, i % 2, :])
                if i + 1 < STEPS:
                    if i:
                        dve.wait_ge(lo_set, i)
                    b_out(i + 1)
                dve.wait_ge(hi_set, i + 1)
                dve.tensor_tensor(b_step, b_step, b_parts[:, i % 2, :, 0, :], ALU.subtract).then_inc(rest1_set, 1)
                dve.wait_ge(mid_set, i + 1)
                dve.tensor_tensor(b_parts[:, i % 2, :, 2, :], b_step, b_parts[:, i % 2, :, 1, :], ALU.subtract).then_inc(lo_set, 1)

            dve.wait_ge(table_stored, 32 * STEPS)
            dve.memset(aggrT[:, :], 0.0)
            dve.memset(ring[:, (SLOTS - LAG) * TILES:, :], 0.0)
            dve.memset(ps_z[1], 0.0)
            dve.wait_ge(consts_set, 5)
            dve.wait_ge(b_set, STEPS)
            dve.tensor_copy(iota, iota_sb[:, :]).then_inc(edge_ready, 1)
            dve.wait_ge(edge_ready, 1)
            dve.sem_inc(onehot_set, LEAD - 1)
            dve.sem_inc(z_added, LEAD - 2)
            dve.sem_inc(score_set, LEAD - 2)
            dve.sem_inc(aggr_set, LEAD - 3)

            def score_group(at, k):
                dve.wait_ge(groups_ready, at(k))
                dve.wait_ge(z_psum, at(k))
                add_a(dve, k % 2, k % SLOTS).then_inc(z_added, 1)
                dve.wait_ge(z_added, at(k))
                score_edges(dve, k % 2).then_inc(score_set, 1)

            def add_group(at, k, group):
                first = dve.value_load(first_row[0:1, ds(group + LAG, 1)], min_val=0, max_val=BIG)
                dve.wait_ge(sum_psum, at(k))
                dve.wait_ge(aggr_set, at(k - 1))
                add_sums(dve, k % 2, first).then_inc(aggr_set, 1)

            with dve.Fori(0, ROUNDS) as r:
                at = counts(dve, r)
                for k in range(SLOTS):
                    dve.wait_ge(weighted_set, at(k - 4))
                    spread_onehot(dve, dst_in[:, ds(r * (SLOTS * TILES) + k * TILES, TILES)], onehot[:, k % 4]).then_inc(onehot_set, 1)
                    score_group(at, k - 1)
                    add_group(at, k - 2, r * SLOTS + (k - 2))
            tail = lambda k: GROUPS + k + LEAD
            score_group(tail, -1)
            add_group(tail, -2, GROUPS - 2)
            add_group(tail, -1, GROUPS - 1)
            dve.wait_ge(aggr_set, tail(-1))
            dve.sem_inc(edges_done, 1)

            any_more = dve.value_load(most_more[0:1, 0:1], min_val=0, max_val=BLOCKS)
            with dve.If(any_more > 0):
                done = dve.alloc_register("dve_done")
                dve.reg_mov(done, 1)
                with dve.Fori(0, GROUPS) as g:
                    first = dve.value_load(first_row[0:1, ds(g + LAG, 1)], min_val=0, max_val=BIG)
                    last = dve.value_load(last_window[0:1, ds(g, 1)], min_val=2, max_val=BLOCKS)
                    with dve.Fori(1, last) as w:
                        n = dve.snap(done, min_val=1, max_val=GROUPS * BLOCKS)
                        dve.tensor_scalar(shifted[:, :], dst_in[:, ds(g * TILES, TILES)], shifts[:, ds(w, 1)], None, ALU.subtract).then_inc(more["shifted"], 1)
                        dve.wait_ge(more["shifted"], n)
                        spread_onehot(dve, shifted[:, :], onehot[:, 0]).then_inc(more["onehot"], 1)
                        dve.wait_ge(more["z_psum"], n)
                        dve.wait_ge(more["gathered"], (g + 1) * (16 * TILES))
                        add_a(dve, 0, 0).then_inc(more["z_added"], 1)
                        dve.wait_ge(more["z_added"], n)
                        score_edges(dve, 0).then_inc(more["score"], 1)
                        dve.wait_ge(more["sum_psum"], n)
                        at_node = dve.snap((first + w * P).with_bounds(min_val=0, max_val=BIG + P))
                        add_sums(dve, 0, at_node).then_inc(more["aggr"], 1)
                        dve.wait_ge(more["aggr"], n + 1)
                        dve.reg_add(done, done, 1)
            dve.sem_inc(all_done, 1)

            for i in range(STEPS):
                dve.wait_ge(aggr_psum, i + 1)
                if i:
                    dve.wait_ge(mixed, i)
                dve.tensor_tensor(grid(tmp[:, :]), grid(ps_x), at_step(h_all, i), ALU.subtract).then_inc(diff_set, 1)
                dve.wait_ge(gate_psum, i + 1)
                dve.tensor_tensor(grid(ps_a), grid(ps_a), step_bc(bg_bc), ALU.add).then_inc(gate_in, 1)
                if i:
                    statistics(h_all, i - 1, mv2_set, STEPS + i - 1)
                dve.wait_ge(diff_set, i + 1)
                dve.wait_ge(gate_set, i + 1)
                dve.tensor_tensor(tmp[:, :], tmp[:, :], gate[:, :], ALU.mult).then_inc(gated, 1)
                dve.wait_ge(gated, i + 1)
                dve.tensor_tensor(at_step(h_all, i), grid(tmp[:, :]), at_step(h_all, i), ALU.add).then_inc(mixed, 1)
            dve.wait_ge(mixed, STEPS)
            statistics(h_all, STEPS - 1, mv2_set, 2 * STEPS - 1)

            dve.wait_ge(sd2_set, 1)
            dve.reciprocal(rstd[:, :], sd[:, :]).then_inc(rstd_set, 1)
            dve.wait_ge(rstd_set, 2)
            dve.wait_ge(xb_set, STEPS)
            for i in range(STEPS):
                normalise(h_all, i, g2_bc, lambda b: x_all[:, b, :], STEPS + i + 1, y_set)
            for i in range(STEPS):
                dve.wait_ge(y_set, i + 1)
                statistics(h_all, i, mv3_set, 2 * STEPS + i)
            dve.wait_ge(sd3_set, 1)
            dve.reciprocal(rstd[:, :], sd[:, :]).then_inc(rstd_set, 1)
            dve.wait_ge(rstd_set, 3)
            for i in range(STEPS):
                for b in range(i * STEP, (i + 1) * STEP):
                    last = dve.tensor_scalar(h_all[:, b, :], h_all[:, b, :], mv[:, b, 0:1], rstd[:, b:b + 1], ALU.subtract, ALU.mult)
                last.then_inc(out_set, 1)


_INS = ["x", "src", "dst", "L0_gnn_W1", "L0_gnn_b1", "L0_gnn_g1", "L0_gnn_bt1", "L0_gnn_We1", "L0_gnn_be1", "L0_gnn_We2",
        "L0_gnn_be2", "L0_gnn_Wg", "L0_gnn_bg", "L0_gnn_g2", "L0_gnn_bt2"]


def kernel(**inputs):
    import numpy as _np
    import concourse.bacc as _bacc
    from concourse import mybir as _mybir
    from concourse.bass_utils import run_bass_kernel_spmd as _run

    nc = _bacc.Bacc("TRN2", target_bir_lowering=False, num_devices=1)
    arrays, args = {}, []
    for name in _INS:
        a = _np.ascontiguousarray(inputs[name])
        arrays[f"in_{name}_dram"] = a
        args.append(nc.dram_tensor(f"in_{name}_dram", a.shape, _mybir.dt.from_np(a.dtype), kind="ExternalInput").ap())
    args.append(nc.dram_tensor("out_0_dram", arrays["in_x_dram"].shape, _mybir.dt.float32, kind="ExternalOutput").ap())
    gnn_layer(nc, *args)
    r = _run(nc, [arrays], core_ids=[0])
    return r.results[0]["out_0_dram"]
```

```python
import concourse.bass as bass
from concourse import mybir
from contextlib import ExitStack


def gnn_layer(nc, x, src, dst, W1, b1, g1, bt1, We1, be1, We2, be2, Wg, bg, g2, bt2, out):
    f32, bf16, i32, u32 = mybir.dt.float32, mybir.dt.bfloat16, mybir.dt.int32, mybir.dt.uint32
    ALU, ACT, AX = mybir.AluOpType, mybir.ActivationFunctionType, mybir.AxisListType.X
    ds = bass.ds

    P = 128
    EPS = 1e-5
    N, D = x.shape
    E = src.shape[0]
    BLOCKS = -(-N // P)
    LAST = N - (BLOCKS - 1) * P
    STEP = 7
    STEPS = BLOCKS // STEP
    assert D == P and STEPS * STEP == BLOCKS and 96 < LAST < P
    BIG = P * BLOCKS - 1
    W = STEP * D

    TILES = 4
    SLOTS = 8
    HALF = SLOTS // 2
    AHEAD = 6
    GE = TILES * P
    GROUPS = -(-E // (GE * SLOTS)) * SLOTS
    ROUNDS = GROUPS // SLOTS
    RW = 2048
    RT, RG = RW // P, RW // GE
    ROWS = GROUPS * GE // RW
    FULL = E // RW
    REST = E - FULL * RW
    assert ROWS * RW == GROUPS * GE and 96 < ROWS <= P and FULL == ROWS - 1 and REST
    STAGED = HALF * TILES
    EDGE_TILES = GROUPS * TILES
    WINDOWS = 4
    B_AHEAD = 3
    B_STEPS = 4
    H_PART = 5
    OUT_PART = 3
    SPLIT = 5
    LAG = 2
    NODES = (BLOCKS + 2) * P

    ctx = ExitStack()
    with ctx:
        def sb(name, shape, dt=f32):
            return ctx.enter_context(nc.sbuf_tensor(name, shape, dt))

        def sem(name):
            return ctx.enter_context(nc.semaphore(name))

        table = nc.dram_tensor("node_table", [BLOCKS * P, 2 * D], f32)
        b_table = nc.dram_tensor("b_table", [NODES, 3 * D], bf16)
        first_dram = nc.dram_tensor("first_dram", [1, GROUPS], f32)

        x_all = sb("x_all", [P, BLOCKS, D])
        h_all = sb("h_all", [P, BLOCKS, D])
        hT_all = sb("hT_all", [P, BLOCKS * P])
        aggrT = sb("aggrT", [P, NODES])
        a_all = aggrT[:, 0:BLOCKS * D].rearrange("p (b f) -> p b f", f=D)
        src_idx = sb("src_idx", [P, EDGE_TILES + SLOTS * TILES], i32)
        dst_in = sb("dst_in", [P, EDGE_TILES])
        region = sb("region", [P, SLOTS * TILES * 2 * D])
        src_rows = region[0:ROWS, 0:RW].bitcast(i32)
        dst_rows = region[0:ROWS, RW:2 * RW].bitcast(i32)
        src_rows_f = region[0:ROWS, 2 * RW:3 * RW]
        dst_rows_f = region[0:ROWS, 3 * RW:4 * RW]
        ring = region[:, :].rearrange("p (t f) -> p t f", f=2 * D)
        gates = region[:, 0:BLOCKS * P]
        idx_stage = sb("idx_stage", [P, 2, STAGED], i32)
        b_window = sb("b_window", [P, WINDOWS, 3, D], bf16)
        onehot = sb("onehot", [P, 4, TILES, P], bf16)
        onehotT = sb("onehotT", [P, 2, TILES, P], bf16)
        weighted = sb("weighted", [P, 2, TILES, P])
        score = sb("score", [P, 2, TILES])
        weight = sb("weight", [P, 2, TILES])
        relu_dot = sb("relu_dot", [P, 2, TILES, D], bf16)
        shifted = sb("shifted", [P, TILES])
        xT = sb("xT", [P, 2, W])
        b_f = xT
        b_parts = sb("b_parts", [P, B_STEPS, STEP, 3, D], bf16)
        stats = sb("stats", [P, 2, STEP, 6])
        mv = sb("mv", [P, BLOCKS, 2])
        sd = sb("sd", [P, BLOCKS])
        rstd = sb("rstd", [P, BLOCKS])
        shift = sb("shift", [P, BLOCKS])
        ident = sb("ident", [P, P])
        ident_bf = sb("ident_bf", [P, P], bf16)
        iota_sb = sb("iota_sb", [P, P])
        shifts = sb("shifts", [P, BLOCKS + 1])
        eps = sb("eps", [P, 1])
        w1_sb = sb("w1_sb", [P, D])
        we1_sb = sb("we1_sb", [P, 2 * D])
        wg_sb = sb("wg_sb", [P, 2, D])
        b1_bc, be1_bc, we2_bc, g2_bc, bt2_bc = (sb(n, [P, D]) for n in ("b1_bc", "be1_bc", "we2_bc", "g2_bc", "bt2_bc"))
        g1_col, bt1_col, bg_col = (sb(n, [P, 1]) for n in ("g1_col", "bt1_col", "bg_col"))
        be2_bc = sb("be2_bc", [P, 1])
        least = sb("least", [P, RG])
        greatest = sb("greatest", [P, RG])
        first_int = sb("first_int", [P, RG], i32)
        span_int = sb("span_int", [P, RG], i32)
        first_row = sb("first_row", [1, LAG + GROUPS + B_AHEAD], i32)
        more_row = sb("more_row", [1, GROUPS], i32)
        most_more = sb("most_more", [1, 1], i32)
        last_window = sb("last_window", [1, GROUPS], i32)
        first_bc = sb("first_bc", [P, GROUPS])

        psum = ctx.enter_context(nc.psum_tensor("psum", [P, 4096], f32))
        BANK = 512
        ps_pair = [psum[:, 2 * i * BANK:2 * i * BANK + W] for i in range(4)]
        ps_x, ps_pre, ps_a, ps_h = ps_pair
        ps_b = [ps_pair[3], ps_pair[2]]
        ps_gate, ps_mix = ps_pair[0:2], ps_pair[2:4]
        ps_onehotT = [psum[:, i * BANK:(i + 1) * BANK].bitcast(bf16)[:, 0:GE].rearrange("p (t n) -> p t n", n=P) for i in range(2)]
        ps_z = [psum[:, (2 + i) * BANK:(3 + i) * BANK].rearrange("p (t f) -> p t f", f=D) for i in range(2)]
        ps_sum = [psum[:, (4 + i) * BANK:(4 + i) * BANK + P] for i in range(2)]
        iota = psum[:, 6 * BANK:6 * BANK + P]

        x_in = [sem(f"x_in{i}") for i in range(STEPS)]
        src_loaded = sem("src_loaded")
        dst_loaded = sem("dst_loaded")
        params_in = sem("params_in")
        pads_set = sem("pads_set")
        spread_zeroed = sem("spread_zeroed")
        consts_zeroed = sem("consts_zeroed")
        consts_set = sem("consts_set")
        ident_bf_set = sem("ident_bf_set")
        src_cast = sem("src_cast")
        dst_cast = sem("dst_cast")
        cols_T = sem("cols_T")
        cols_out = sem("cols_out")
        extremes_set = sem("extremes_set")
        first_set = sem("first_set")
        span_set = sem("span_set")
        rows_in = sem("rows_in")
        bc_moved = sem("bc_moved")
        bc_in = sem("bc_in")
        more_set = sem("more_set")
        local_set = sem("local_set")
        xT_psum = sem("xT_psum")
        xT_set = sem("xT_set")
        pre_psum = sem("pre_psum")
        pre_set = sem("pre_set")
        stats_set = sem("stats_set")
        mv_set = sem("mv_set")
        sd_set = sem("sd_set")
        rstd_set = sem("rstd_set")
        shift_set = sem("shift_set")
        normed = sem("normed")
        normed_rest = sem("normed_rest")
        normedT_psum = sem("normedT_psum")
        hT_set = sem("hT_set")
        h_psum = sem("h_psum")
        h_set = sem("h_set")
        a_psum = sem("a_psum")
        a_set = sem("a_set")
        b_psum = sem("b_psum")
        table_stored = sem("table_stored")
        hi_set = sem("hi_set")
        rest1_set = sem("rest1_set")
        mid_set = sem("mid_set")
        lo_set = sem("lo_set")
        aggr_begun = sem("aggr_begun")
        wsum_set = sem("wsum_set")
        edge_ready = sem("edge_ready")
        edges_done = sem("edges_done")
        all_done = sem("all_done")
        b_padded = sem("b_padded")
        b_stored = [sem(f"b_stored{i}") for i in range(B_STEPS)]
        first_params_in = sem("first_params_in")
        xb_set = sem("xb_set")
        idx_staged = [sem(f"idx_staged{i}") for i in range(2)]
        gathered = [sem(f"gathered{i}") for i in range(SLOTS)]
        b_loaded = [sem(f"b_loaded{i}") for i in range(WINDOWS)]
        groups_ready = sem("groups_ready")
        slots_free = sem("slots_free")
        pool_turn = sem("pool_turn")
        onehot_set = sem("onehot_set")
        onehotT_psum = sem("onehotT_psum")
        onehotT_set = sem("onehotT_set")
        z_psum = sem("z_psum")
        z_added = sem("z_added")
        score_set = sem("score_set")
        weight_set = sem("weight_set")
        weighted_set = sem("weighted_set")
        sum_psum = sem("sum_psum")
        aggr_set = sem("aggr_set")
        more = {n: sem("more_" + n) for n in ("staged", "gathered", "b_loaded", "shifted", "onehot", "onehotT_psum", "onehotT",
                                              "z_psum", "z_added", "score", "weight", "weighted", "sum_psum", "aggr")}
        gate_psum = sem("gate_psum")
        gate_set = sem("gate_set")
        gated = sem("gated")
        gated_psum = sem("gated_psum")
        mixed = sem("mixed")
        mv2_set = sem("mv2_set")
        sd2_set = sem("sd2_set")
        shift2_set = sem("shift2_set")
        normed2 = sem("normed2")
        scaled2 = sem("scaled2")
        y_set = sem("y_set")
        mv3_set = sem("mv3_set")
        sd3_set = sem("sd3_set")
        shift3_set = sem("shift3_set")
        out_set = sem("out_set")
        out_rest_set = sem("out_rest_set")
        stored = sem("stored")

        LEAD = 5
        PARAMS = 10

        def steps(t, i):
            return t[:, ds(i * STEP, STEP)]

        def at_step(t, i):
            return t[:, i * STEP:(i + 1) * STEP]

        def columns(t, i):
            return t[:, i * W:(i + 1) * W]

        def list_columns(n):
            q = n % 4
            return psum[:, BANK * q:BANK * q + 4 * ROWS].rearrange("q (j p) -> q j p", j=4)

        def step_bc(v):
            return v[:, :].unsqueeze(1).to_broadcast([P, STEP, D])

        def grid(t):
            return t.rearrange("p (b f) -> p b f", f=D)

        def ring_a(slot):
            return ring[:, slot * TILES:(slot + 1) * TILES, 0:D]

        def counts(eng, r):
            held = {k: eng.snap(r * SLOTS + (k + LEAD), min_val=1, max_val=GROUPS + LEAD) for k in range(-4, SLOTS)}
            return held.__getitem__

        def spread_onehot(eng, g_local, out_onehot):
            return eng.tensor_tensor(out_onehot, iota.unsqueeze(1).to_broadcast([P, TILES, P]),
                                     g_local.unsqueeze(2).to_broadcast([P, TILES, P]), ALU.is_equal)

        def transpose_onehot(eng, i_onehot, i):
            for t in range(TILES):
                last = eng.transpose(ps_onehotT[i][:, t, :], onehot[:, i_onehot, t, :], ident_bf[:, :])
            return last

        def spread_b(eng, i, window):
            for t in range(TILES):
                for k in range(3):
                    last = eng.matmul(ps_z[i][:, t, :], onehotT[:, i, t, :], b_window[:, window, k, :], start=(k == 0), stop=(k == 2))
            return last

        def add_a(eng, i, slot):
            return eng.tensor_tensor(ps_z[i], ps_z[i], ring_a(slot), ALU.add)

        def score_edges(eng, i):
            for t in range(TILES):
                last = eng.scalar_tensor_tensor(relu_dot[:, i, t, :], ps_z[i][:, t, :], 0.0, we2_bc[:, :], ALU.max, ALU.mult,
                                                accum_out=score[:, i, t:t + 1])
            return last

        def sigmoid_score(eng, i):
            return eng.activation(weight[:, i, :], score[:, i, :], ACT.Sigmoid, bias=be2_bc[:, 0:1])

        def weigh(eng, i, i_onehot):
            for t in range(TILES):
                last = eng.activation(weighted[:, i, t, :], onehot[:, i_onehot, t, :], ACT.Copy, scale=weight[:, i, t:t + 1])
            return last

        def sum_rows(eng, i, slot):
            for t in range(TILES):
                last = eng.matmul(ps_sum[i], ring[:, slot * TILES + t, D:2 * D], weighted[:, i, t, :], start=(t == 0), stop=(t == TILES - 1))
            return last

        def add_sums(eng, i, first):
            return eng.tensor_tensor(aggrT[:, ds(first, P)], aggrT[:, ds(first, P)], ps_sum[i], ALU.add)

        block = ctx.enter_context(nc.Block())

        @block.sync
        def _(sp):
            x_blocks = x[0:(BLOCKS - 1) * P, :].rearrange("(b p) f -> p b f", p=P)
            for i in range(STEPS):
                n = STEP if i < STEPS - 1 else STEP - 1
                sp.dma_start(x_all[:, i * STEP:i * STEP + n, :],
                             x_blocks[:, i * STEP:i * STEP + n, :]).then_inc(x_in[i], 16)
            sp.wait_ge(pads_set, 4)
            sp.dma_start(x_all[0:LAST, BLOCKS - 1, :], x[(BLOCKS - 1) * P:N, :]).then_inc(x_in[STEPS - 1], 16)
            sp.wait_ge(pads_set, 2)
            for rows, edges, loaded in ((dst_rows, dst, dst_loaded), (src_rows, src, src_loaded)):
                sp.dma_start(rows[0:FULL, :], edges[0:FULL * RW].rearrange("(p e) -> p e", e=RW)).then_inc(loaded, 16)
                sp.dma_start(rows[FULL:ROWS, 0:REST], edges[FULL * RW:E].rearrange("(p e) -> p e", p=1)).then_inc(loaded, 16)
            sp.dma_start(bg_col[:, :], bg.rearrange("(f o) -> f o", o=1)).then_inc(params_in, 16)
            for dst_bc, v in ((be1_bc, be1), (we2_bc, We2.rearrange("f o -> (f o)")), (g2_bc, g2), (bt2_bc, bt2), (be2_bc, be2)):
                n = v.shape[0]
                sp.dma_start(dst_bc[:, :], v.rearrange("(o f) -> o f", o=1).to_broadcast([P, n])).then_inc(params_in, 16)
            sp.dma_start(wg_sb[:, :, :], Wg.rearrange("(c k) f -> k c f", c=2)).then_inc(params_in, 16)
            tab = table[:, :].rearrange("(b p) f -> p b f", p=P)

            def store_table(i):
                sp.wait_ge(h_set, i + 1)
                sp.dma_start(steps(tab, i)[:, :, D:2 * D], steps(h_all, i)).then_inc(table_stored, 16)
                sp.wait_ge(a_set, i + 1)
                sp.dma_start(steps(tab, i)[:, :, 0:D], steps(a_all, i)).then_inc(table_stored, 16)

            with sp.Fori(0, STEPS - 1) as i:
                store_table(i)
            sp.wait_ge(cols_out, 4)
            for half in range(2):
                sp.dma_start(idx_stage[:, half, :], src_idx[:, half * STAGED:(half + 1) * STAGED]).then_inc(idx_staged[half], 16)
            sp.sem_inc(slots_free, AHEAD)
            sp.wait_ge(first_set, 2)
            sp.dma_start(first_row[0:1, LAG:LAG + GROUPS], first_int[0:ROWS, :]).then_inc(rows_in, 16)
            sp.dma_start(first_dram[0:1, :].rearrange("o (p g) -> (o p) g", g=RG), least[0:ROWS, :]).then_inc(bc_moved, 16)
            sp.wait_ge(span_set, 1)
            sp.dma_start(more_row[0:1, :], span_int[0:ROWS, :]).then_inc(rows_in, 16)
            store_table(STEPS - 1)
            sp.wait_ge(bc_moved, 16)
            sp.dma_start(first_bc[:, :], first_dram[0:1, :].to_broadcast([P, GROUPS])).then_inc(bc_in, 16)
            sp.wait_ge(spread_zeroed, 1)
            for i in range(2):
                sp.dma_start(b_table[(BLOCKS + i) * P:(BLOCKS + i + 1) * P, :].rearrange("p (k f) -> p k f", k=3), onehot[:, i, 0:3, :]).then_inc(b_padded, 16)
            b_tab = b_table[0:BLOCKS * P, :].rearrange("(b p) (k f) -> p b k f", p=P, k=3)
            for i in range(STEPS):
                sp.wait_ge(lo_set, i + 1)
                sp.dma_start(b_tab[:, i * STEP:(i + 1) * STEP], b_parts[:, i % B_STEPS]).then_inc(b_stored[i % B_STEPS], 16)

            def load_window(group, window):
                first = sp.value_load(first_row[0:1, ds(group + LAG, 1)], min_val=0, max_val=BIG)
                sp.dma_start(b_window[:, window, :, :], b_table[ds(first, P), :].rearrange("p (k f) -> p k f", k=3)).then_inc(b_loaded[window], 16)

            sp.wait_ge(rows_in, 32)
            sp.wait_ge(b_padded, 32)
            for i in range(B_STEPS):
                sp.wait_ge(b_stored[i], 16 * len(range(i, STEPS, B_STEPS)))
            sp.sem_inc(groups_ready, LEAD - 1)
            for g in range(B_AHEAD):
                load_window(g, g)
            with sp.Fori(0, ROUNDS) as r:
                at = counts(sp, r)
                for k in range(SLOTS):
                    sp.wait_ge(gathered[k], (r + 1) * (16 * TILES))
                    sp.sem_inc(groups_ready, 1)
                    if k % HALF == HALF - 1:
                        half = k // HALF
                        sp.dma_start(idx_stage[:, half, :],
                                     src_idx[:, ds((r + 1) * (SLOTS * TILES) + half * STAGED, STAGED)]).then_inc(idx_staged[half], 16)
                    sp.wait_ge(sum_psum, at(k + AHEAD - SLOTS))
                    sp.sem_inc(slots_free, 1)
                    sp.wait_ge(z_psum, at(k - 1))
                    load_window(r * SLOTS + (k + B_AHEAD), (k + B_AHEAD) % WINDOWS)
            for half in range(2):
                sp.wait_ge(idx_staged[half], 16 * (ROUNDS + 1))
            for j in range(WINDOWS):
                sp.wait_ge(b_loaded[j], 16 * (GROUPS // WINDOWS + (j < B_AHEAD)))

            sp.wait_ge(more_set, 1)
            any_more = sp.value_load(most_more[0:1, 0:1], min_val=0, max_val=BLOCKS)
            with sp.If(any_more > 0):
                sp.wait_ge(edges_done, 1)
                done = sp.alloc_register("sp_done")
                sp.reg_mov(done, 1)
                sp.sem_inc(more["aggr"], 1)
                with sp.Fori(0, GROUPS) as g:
                    n = sp.snap(done, min_val=1, max_val=GROUPS * BLOCKS)
                    sp.wait_ge(more["aggr"], n)
                    sp.dma_start(idx_stage[:, 0, 0:TILES], src_idx[:, ds(g * TILES, TILES)]).then_inc(more["staged"], 16)
                    first = sp.value_load(first_row[0:1, ds(g + LAG, 1)], min_val=0, max_val=BIG)
                    last = sp.value_load(last_window[0:1, ds(g, 1)], min_val=2, max_val=BLOCKS)
                    with sp.Fori(1, last) as w:
                        n = sp.snap(done, min_val=1, max_val=GROUPS * BLOCKS)
                        sp.wait_ge(more["aggr"], n)
                        at_node = sp.snap((first + w * P).with_bounds(min_val=0, max_val=BIG + P))
                        sp.dma_start(b_window[:, 0, :, :], b_table[ds(at_node, P), :].rearrange("p (k f) -> p k f", k=3)).then_inc(more["b_loaded"], 16)
                        sp.reg_add(done, done, 1)

            out_blocks = out[0:(BLOCKS - 1) * P, :].rearrange("(b p) f -> p b f", p=P)
            with sp.Fori(0, STEPS - 1) as i:
                sp.wait_ge(out_set, i + 1)
                sp.wait_ge(out_rest_set, i + 1)
                sp.dma_start(steps(out_blocks, i), steps(h_all, i)).then_inc(stored, 16)
            sp.wait_ge(out_set, STEPS)
            sp.wait_ge(out_rest_set, STEPS)
            sp.dma_start(out_blocks[:, (STEPS - 1) * STEP:BLOCKS - 1, :], h_all[:, (STEPS - 1) * STEP:BLOCKS - 1, :]).then_inc(stored, 16)
            sp.dma_start(out[(BLOCKS - 1) * P:N, :], h_all[0:LAST, BLOCKS - 1, :]).then_inc(stored, 16)
            sp.wait_ge(stored, 16 * (STEPS + 1))

        @block.gpsimd
        def _(pool):
            pool.memset(src_idx[:, EDGE_TILES:], 0).then_inc(consts_set, 1)
            pool.memset(ident[:, :], 0.0).then_inc(consts_zeroed, 1)
            pool.memset(eps[:, :], EPS).then_inc(consts_set, 1)
            pool.iota(iota_sb[:, :], pattern=[[1, P]], base=0, channel_multiplier=0,
                      allow_small_or_imprecise_dtypes=True).then_inc(consts_set, 1)
            pool.iota(shifts[:, :], pattern=[[P, BLOCKS + 1]], base=0, channel_multiplier=0,
                      allow_small_or_imprecise_dtypes=True).then_inc(consts_set, 1)
            pool.wait_ge(consts_zeroed, 1)
            pool.affine_select(out=ident[:, :], in_=ident[:, :], compare_op=ALU.not_equal, fill=1.0,
                               base=0, pattern=[[-1, P]], channel_multiplier=1).then_inc(consts_set, 1)
            pool.memset(weighted[:, :, :, :], 0.0)
            pool.memset(onehot[:, :, :, :], 0.0).then_inc(spread_zeroed, 1)
            pool.wait_ge(src_loaded, 32)
            pool.tensor_copy(src_rows_f, src_rows).then_inc(src_cast, 1)

            pool.wait_ge(params_in, 16 * PARAMS)
            with pool.Fori(0, STEPS) as i:
                pool.wait_ge(xT_psum, i + 1)
                pool.tensor_tensor(steps(x_all, i), steps(x_all, i), step_bc(bt2_bc), ALU.add).then_inc(xb_set, 1)

            pool.wait_ge(table_stored, 32 * STEPS)
            pool.wait_ge(cols_T, 8)
            with pool.Fori(0, ROUNDS) as r:
                for k in range(SLOTS):
                    half, c = k // HALF, (k % HALF) * TILES
                    if k % HALF == 0:
                        pool.wait_ge(idx_staged[half], (r + 1) * 16)
                    pool.wait_ge(slots_free, r * SLOTS + (k + 1))
                    pool.sem_inc(pool_turn, 1)
                    for t in range(TILES):
                        pool.indirect_dma_start(
                            out=ring[:, k * TILES + t, :], out_offset=None, in_=table[:, :],
                            in_offset=bass.IndirectOffsetOnAxis(ap=idx_stage[:, half, c + t:c + t + 1].bitcast(u32), axis=0),
                        ).then_inc(gathered[k], 16)

            pool.wait_ge(more_set, 1)
            any_more = pool.value_load(most_more[0:1, 0:1], min_val=0, max_val=BLOCKS)
            with pool.If(any_more > 0):
                with pool.Fori(0, GROUPS) as g:
                    pool.wait_ge(more["staged"], (g + 1) * 16)
                    pool.sem_inc(pool_turn, 1)
                    for t in range(TILES):
                        pool.indirect_dma_start(
                            out=ring[:, t, :], out_offset=None, in_=table[:, :],
                            in_offset=bass.IndirectOffsetOnAxis(ap=idx_stage[:, 0, t:t + 1].bitcast(u32), axis=0),
                        ).then_inc(more["gathered"], 16)

            pool.wait_ge(xb_set, STEPS)
            with pool.Fori(0, STEPS) as i:
                pool.wait_ge(scaled2, i + 1)
                pool.tensor_tensor(steps(h_all, i), steps(h_all, i), steps(x_all, i), ALU.add).then_inc(y_set, 1)

        @block.scalar
        def _(act):
            act.dma_start(w1_sb[:, :], W1[:, :]).then_inc(first_params_in, 16)
            act.dma_start(b1_bc[:, :], b1.rearrange("(o f) -> o f", o=1).to_broadcast([P, D])).then_inc(first_params_in, 16)
            act.dma_start(we1_sb[:, :].rearrange("k (c f) -> k c f", c=2), We1.rearrange("(c k) f -> k c f", c=2)).then_inc(params_in, 16)
            for col, v in ((g1_col, g1), (bt1_col, bt1)):
                act.dma_start(col[:, :], v.rearrange("(f o) -> f o", o=1)).then_inc(params_in, 16)
            act.preload_act_table(ACT.Sqrt)
            act.wait_ge(consts_set, 5)
            act.activation(ident_bf[:, :], ident[:, :], ACT.Copy).then_inc(ident_bf_set, 1)

            def xT_out(i):
                act.wait_ge(xT_psum, i + 1)
                act.activation(xT[:, i % 2, :], ps_x, ACT.Copy).then_inc(xT_set, 1)

            def deviations(b0, b1):
                return act.activation(sd[:, b0:b1], mv[:, b0:b1, 1], ACT.Sqrt, bias=eps[:, 0:1])

            def normalise(i, n):
                for b in range(i * STEP, i * STEP + n):
                    last = act.activation(h_all[:, b, :], h_all[:, b, :], ACT.Identity, bias=shift[:, b:b + 1], scale=rstd[:, b:b + 1])
                return last

            xT_out(0)
            for turn in range(STEPS + 2):
                i = turn - 2
                if i >= 0:
                    act.wait_ge(params_in, 16 * PARAMS)
                    act.wait_ge(normedT_psum, i + 1)
                    act.activation(columns(hT_all, i), ps_h, ACT.Relu, bias=bt1_col[:, 0:1], scale=g1_col[:, 0:1]).then_inc(hT_set, 1)
                if turn + 1 < STEPS:
                    xT_out(turn + 1)
                if 1 <= turn <= STEPS:
                    act.wait_ge(shift_set, turn)
                    normalise(turn - 1, H_PART).then_inc(normed, 1)
                if i >= 0:
                    act.wait_ge(h_psum, i + 1)
                    act.activation(at_step(h_all, i), grid(ps_h), ACT.Copy).then_inc(h_set, 1)
                if turn < STEPS:
                    act.wait_ge(mv_set, turn + 1)
                    deviations(turn * STEP, (turn + 1) * STEP).then_inc(sd_set, 1)
                if turn == STEPS:
                    act.wait_ge(dst_loaded, 32)
                    act.activation(dst_rows_f, dst_rows, ACT.Copy).then_inc(dst_cast, 1)

            def middle(i):
                act.wait_ge(rest1_set, i + 1)
                act.activation(b_parts[:, i % B_STEPS, :, 1, :], grid(b_f[:, i % 2, :]), ACT.Copy).then_inc(mid_set, 1)

            for i in range(STEPS):
                act.wait_ge(b_psum, i + 1)
                if i >= B_STEPS:
                    act.wait_ge(b_stored[i % B_STEPS], 16 * (i // B_STEPS))
                act.activation(b_parts[:, i % B_STEPS, :, 0, :], grid(ps_b[i % 2]), ACT.Copy).then_inc(hi_set, 1)
                if i:
                    middle(i - 1)
            middle(STEPS - 1)
            act.wait_ge(table_stored, 32 * STEPS)
            with act.Fori(0, STEPS) as i:
                act.activation(aggrT[:, ds(i * W, W)], hT_all[:, ds(i * W, W)], ACT.Copy, scale=-1.0).then_inc(aggr_begun, 1)

            act.preload_act_table(ACT.Sigmoid)
            act.sem_inc(onehotT_set, LEAD - 1)
            act.sem_inc(weight_set, LEAD - 2)
            act.sem_inc(weighted_set, LEAD - 2)

            def weigh_group(at, k):
                act.wait_ge(score_set, at(k))
                sigmoid_score(act, k % 2).then_inc(weight_set, 1)
                act.wait_ge(weight_set, at(k))
                act.wait_ge(sum_psum, at(k - 2))
                weigh(act, k % 2, k % 4).then_inc(weighted_set, 1)

            with act.Fori(0, ROUNDS) as r:
                at = counts(act, r)
                for k in range(SLOTS):
                    act.wait_ge(onehotT_psum, at(k))
                    act.wait_ge(z_psum, at(k - 2))
                    act.activation(onehotT[:, k % 2], ps_onehotT[k % 2], ACT.Copy).then_inc(onehotT_set, 1)
                    weigh_group(at, k - 1)
            weigh_group(lambda k: GROUPS + k + LEAD, -1)

            act.wait_ge(more_set, 1)
            any_more = act.value_load(most_more[0:1, 0:1], min_val=0, max_val=BLOCKS)
            with act.If(any_more > 0):
                done = act.alloc_register("act_done")
                act.reg_mov(done, 1)
                with act.Fori(0, GROUPS) as g:
                    last = act.value_load(last_window[0:1, ds(g, 1)], min_val=2, max_val=BLOCKS)
                    with act.Fori(1, last) as w:
                        n = act.snap(done, min_val=1, max_val=GROUPS * BLOCKS)
                        act.wait_ge(more["onehotT_psum"], n)
                        act.activation(onehotT[:, 0], ps_onehotT[0], ACT.Copy).then_inc(more["onehotT"], 1)
                        act.wait_ge(more["score"], n)
                        sigmoid_score(act, 0).then_inc(more["weight"], 1)
                        act.wait_ge(more["weight"], n)
                        weigh(act, 0, 0).then_inc(more["weighted"], 1)
                        act.reg_add(done, done, 1)

            for i in range(STEPS):
                act.wait_ge(gate_psum, i + 1)
                act.activation(columns(gates, i), ps_gate[i % 2], ACT.Sigmoid, bias=bg_col[:, 0:1]).then_inc(gate_set, 1)
            act.wait_ge(mv2_set, SPLIT)
            deviations(0, SPLIT * STEP).then_inc(sd2_set, 1)
            for turn in range(-1, STEPS + 2):
                if turn == 0:
                    act.wait_ge(mv2_set, STEPS)
                    deviations(SPLIT * STEP, BLOCKS).then_inc(sd2_set, 1)
                if turn + 1 < STEPS:
                    act.wait_ge(shift2_set, 1 if turn + 1 < SPLIT else 2)
                    normalise(turn + 1, STEP).then_inc(normed2, 1)
                if turn >= 2:
                    act.wait_ge(shift3_set, turn - 1)
                    normalise(turn - 2, OUT_PART).then_inc(out_set, 1)
                if 1 <= turn <= STEPS:
                    act.wait_ge(mv3_set, turn)
                    deviations((turn - 1) * STEP, turn * STEP).then_inc(sd3_set, 1)

        @block.tensor
        def _(pe):
            pe.wait_ge(consts_set, 5)

            def transpose_list(n):
                rows = src_rows_f if n < 4 else dst_rows_f
                for j in range(4):
                    c = (4 * (n % 4) + j) * P
                    last = pe.transpose(list_columns(n)[:, j, :], rows[:, c:c + P], ident[0:ROWS, 0:ROWS])
                return last

            def transpose_x(i):
                pe.wait_ge(x_in[i], 16 if i < STEPS - 1 else 32)
                if i:
                    pe.wait_ge(xT_set, i)
                for t in range(STEP):
                    last = pe.transpose(ps_x[:, t * P:(t + 1) * P], x_all[:, i * STEP + t, :], ident[:, :])
                last.then_inc(xT_psum, 1)

            def product_x(i):
                pe.wait_ge(xT_set, i + 1)
                if i:
                    pe.wait_ge(pre_set, i)
                for t in range(STEP):
                    last = pe.matmul(ps_pre[:, t * P:(t + 1) * P], xT[:, i % 2, t * P:(t + 1) * P], w1_sb[:, :], start=True, stop=True)
                last.then_inc(pre_psum, 1)

            def transpose_normed(i):
                pe.wait_ge(normed, i + 1)
                pe.wait_ge(normed_rest, i + 1)
                if i:
                    pe.wait_ge(h_set, i)
                for t in range(STEP):
                    last = pe.transpose(ps_h[:, t * P:(t + 1) * P], h_all[:, i * STEP + t, :], ident[:, :])
                last.then_inc(normedT_psum, 1)

            def transpose_h(i):
                pe.wait_ge(hT_set, i + 1)
                for t in range(STEP):
                    b = i * STEP + t
                    last = pe.transpose(ps_h[:, t * P:(t + 1) * P], hT_all[:, b * P:(b + 1) * P], ident[:, :])
                last.then_inc(h_psum, 1)

            def product_h(i, ps, half):
                for t in range(STEP):
                    b = i * STEP + t
                    last = pe.matmul(ps[:, t * D:(t + 1) * D], hT_all[:, b * P:(b + 1) * P], we1_sb[:, half * D:(half + 1) * D], start=True, stop=True)
                return last

            transpose_x(0)
            pe.wait_ge(first_params_in, 32)
            for turn in range(STEPS + 2):
                i = turn - 2
                if i >= 0:
                    transpose_normed(i)
                if turn + 1 < STEPS:
                    transpose_x(turn + 1)
                if turn < STEPS:
                    product_x(turn)
                if turn == STEPS:
                    pe.wait_ge(src_cast, 1)
                    pe.wait_ge(pre_set, STEPS)
                    for n in range(4):
                        transpose_list(n).then_inc(cols_T, 1)
                if turn == STEPS + 1:
                    pe.wait_ge(dst_cast, 1)
                    for n in range(4, 8):
                        pe.wait_ge(cols_out, n - 3)
                        transpose_list(n).then_inc(cols_T, 1)
                if i >= 0:
                    transpose_h(i)
                    if i:
                        pe.wait_ge(a_set, i)
                    else:
                        pe.wait_ge(params_in, 16 * PARAMS)
                    product_h(i, ps_a, 0).then_inc(a_psum, 1)
            for i in range(STEPS):
                if i == 0:
                    pe.wait_ge(h_set, STEPS)
                elif i == 1:
                    pe.wait_ge(a_set, STEPS)
                else:
                    pe.wait_ge(rest1_set, i - 1)
                product_h(i, ps_b[i % 2], 1).then_inc(b_psum, 1)

            pe.sem_inc(onehotT_psum, LEAD - 1)
            pe.sem_inc(z_psum, LEAD - 1)
            pe.sem_inc(sum_psum, LEAD - 3)
            pe.wait_ge(ident_bf_set, 1)
            pe.wait_ge(edge_ready, 1)

            def sum_group(at, k):
                pe.wait_ge(weighted_set, at(k))
                pe.wait_ge(aggr_set, at(k - 2))
                sum_rows(pe, k % 2, k % SLOTS).then_inc(sum_psum, 1)

            with pe.Fori(0, ROUNDS) as r:
                at = counts(pe, r)
                loaded = [pe.snap((r * 2 + j + 1) * 16, min_val=16, max_val=32 * ROUNDS) for j in range(2)]
                for k in range(SLOTS):
                    pe.wait_ge(onehot_set, at(k))
                    pe.wait_ge(onehotT_set, at(k - 2))
                    transpose_onehot(pe, k % 4, k % 2).then_inc(onehotT_psum, 1)
                    sum_group(at, k - 2)
                    pe.wait_ge(score_set, at(k - 2))
                    pe.wait_ge(b_loaded[k % WINDOWS], loaded[k // WINDOWS])
                    pe.wait_ge(onehotT_set, at(k))
                    spread_b(pe, k % 2, k % WINDOWS).then_inc(z_psum, 1)
            for k in (-2, -1):
                sum_group(lambda k: GROUPS + k + LEAD, k)

            pe.wait_ge(more_set, 1)
            any_more = pe.value_load(most_more[0:1, 0:1], min_val=0, max_val=BLOCKS)
            with pe.If(any_more > 0):
                done = pe.alloc_register("pe_done")
                pe.reg_mov(done, 1)
                with pe.Fori(0, GROUPS) as g:
                    last = pe.value_load(last_window[0:1, ds(g, 1)], min_val=2, max_val=BLOCKS)
                    with pe.Fori(1, last) as w:
                        n = pe.snap(done, min_val=1, max_val=GROUPS * BLOCKS)
                        pe.wait_ge(more["onehot"], n)
                        transpose_onehot(pe, 0, 0).then_inc(more["onehotT_psum"], 1)
                        pe.wait_ge(more["onehotT"], n)
                        pe.wait_ge(more["b_loaded"], n * 16)
                        spread_b(pe, 0, 0).then_inc(more["z_psum"], 1)
                        pe.wait_ge(more["weighted"], n)
                        sum_rows(pe, 0, 0).then_inc(more["sum_psum"], 1)
                        pe.reg_add(done, done, 1)

            def transpose_gated(i):
                pe.wait_ge(gated, i + 1)
                if i >= 2:
                    pe.wait_ge(mixed, i - 1)
                for t in range(STEP):
                    b = i * STEP + t
                    last = pe.transpose(ps_mix[i % 2][:, t * P:(t + 1) * P], gates[:, b * P:(b + 1) * P], ident[:, :])
                last.then_inc(gated_psum, 1)

            def gate_half(i, half, of):
                for c, n in ((0, BANK), (BANK, W - BANK)):
                    last = pe.matmul(ps_gate[i % 2][:, c:c + n], wg_sb[:, half, :], of[:, i * W + c:i * W + c + n], start=(half == 0), stop=(half == 1))
                return last

            pe.wait_ge(wsum_set, 1)
            for i in range(2):
                gate_half(i, 0, hT_all)
            pe.wait_ge(all_done, 1)
            for i in range(STEPS):
                if i >= 2:
                    pe.wait_ge(gate_set, i - 1)
                    gate_half(i, 0, hT_all)
                gate_half(i, 1, aggrT).then_inc(gate_psum, 1)
                if i:
                    transpose_gated(i - 1)
            transpose_gated(STEPS - 1)

        @block.vector
        def _(dve):
            dve.memset(dst_rows[96:ROWS, :], BIG).then_inc(pads_set, 1)
            dve.memset(src_rows[96:ROWS, :], 0).then_inc(pads_set, 1)
            dve.memset(x_all[96:P, BLOCKS - 1, :], 0.0).then_inc(pads_set, 1)
            dve.memset(first_row[:, :], 0).then_inc(pads_set, 1)

            def statistics(i, done, n):
                for c in range(STEP):
                    last = dve.bn_stats(stats[:, n % 2, c, :], h_all[:, i * STEP + c, :])
                last.then_inc(stats_set, 1)
                dve.wait_ge(stats_set, n + 1)
                for c in range(STEP):
                    last = dve.bn_aggr(mv[:, i * STEP + c, :], stats[:, n % 2, c, :])
                last.then_inc(done, 1)

            def reciprocals(b0, b1, done, n):
                dve.reciprocal(rstd[:, b0:b1], sd[:, b0:b1]).then_inc(rstd_set, 1)
                dve.wait_ge(rstd_set, n + 1)
                dve.scalar_tensor_tensor(shift[:, b0:b1], mv[:, b0:b1, 0], -1.0, rstd[:, b0:b1], ALU.mult, ALU.mult).then_inc(done, 1)

            def normalise(i, n, done):
                for b in range(i * STEP + n, (i + 1) * STEP):
                    last = dve.tensor_scalar(h_all[:, b, :], h_all[:, b, :], mv[:, b, 0:1], rstd[:, b:b + 1], ALU.subtract, ALU.mult)
                last.then_inc(done, 1)

            def copy_list(n):
                q = n % 4
                dve.wait_ge(cols_T, n + 1)
                cols = (src_idx[:, 0:EDGE_TILES] if n < 4 else dst_in[:, :]).rearrange("q (p j) -> q j p", j=RT)[:, 4 * q:4 * q + 4, :]
                if n < 4:
                    return dve.tensor_copy(cols, list_columns(n))
                first = first_bc[:, :].rearrange("q (p g) -> q g p", g=RG)[:, q:q + 1, :]
                return dve.tensor_tensor(cols, list_columns(n), first.to_broadcast([P, 4, ROWS]), ALU.subtract)

            dve.wait_ge(first_params_in, 32)
            for turn in range(STEPS + 2):
                i = turn - 2
                if turn < STEPS:
                    dve.wait_ge(pre_psum, turn + 1)
                    dve.tensor_tensor(at_step(h_all, turn), grid(ps_pre), step_bc(b1_bc), ALU.add).then_inc(pre_set, 1)
                    dve.wait_ge(pre_set, turn + 1)
                    statistics(turn, mv_set, turn)
                if turn == STEPS:
                    for n in range(4):
                        copy_list(n).then_inc(cols_out, 1)
                if turn == STEPS + 1:
                    dve.wait_ge(dst_loaded, 32)
                    by_group = dst_rows.rearrange("p (g e) -> p g e", e=GE)
                    dve.tensor_reduce(least[0:ROWS, :], by_group, AX, ALU.min).then_inc(first_set, 1)
                    dve.tensor_reduce(greatest[0:ROWS, :], by_group, AX, ALU.max).then_inc(extremes_set, 1)
                    dve.wait_ge(extremes_set, 1)
                    dve.tensor_copy(first_int[0:ROWS, :], least[0:ROWS, :]).then_inc(first_set, 1)
                    dve.tensor_tensor(span_int[0:ROWS, :], greatest[0:ROWS, :], least[0:ROWS, :], ALU.subtract).then_inc(span_set, 1)
                if i >= 0:
                    if i == 0:
                        dve.wait_ge(params_in, 16 * PARAMS)
                    dve.wait_ge(a_psum, i + 1)
                    dve.tensor_tensor(at_step(a_all, i), grid(ps_a), step_bc(be1_bc), ALU.add).then_inc(a_set, 1)
                if turn < STEPS:
                    dve.wait_ge(sd_set, turn + 1)
                    reciprocals(turn * STEP, (turn + 1) * STEP, shift_set, turn)
                    normalise(turn, H_PART, normed_rest)

            dve.tensor_tensor(wg_sb[:, 0, :], wg_sb[:, 0, :], wg_sb[:, 1, :], ALU.add).then_inc(wsum_set, 1)

            def low(i):
                dve.wait_ge(mid_set, i + 1)
                dve.tensor_tensor(b_parts[:, i % B_STEPS, :, 2, :], grid(b_f[:, i % 2, :]), b_parts[:, i % B_STEPS, :, 1, :], ALU.subtract).then_inc(lo_set, 1)

            for i in range(STEPS):
                dve.wait_ge(hi_set, i + 1)
                if i >= 2:
                    dve.wait_ge(lo_set, i - 1)
                dve.tensor_tensor(grid(b_f[:, i % 2, :]), grid(ps_b[i % 2]), b_parts[:, i % B_STEPS, :, 0, :], ALU.subtract).then_inc(rest1_set, 1)
                if i:
                    low(i - 1)
            low(STEPS - 1)

            dve.wait_ge(bc_in, 16)
            for n in range(4, 8):
                copy_list(n).then_inc(cols_out, 1)
            dve.wait_ge(rows_in, 32)
            dve.tensor_scalar(more_row[:, :], more_row[:, :], 7, None, ALU.arith_shift_right).then_inc(local_set, 1)
            dve.wait_ge(local_set, 1)
            dve.tensor_reduce(most_more[:, :], more_row[:, :], AX, ALU.max)
            dve.tensor_scalar(last_window[:, :], more_row[:, :], 1.0, 1.0, ALU.max, ALU.add).then_inc(more_set, 1)
            dve.memset(ring[:, (SLOTS - LAG) * TILES:, :], 0.0)
            dve.memset(aggrT[:, BLOCKS * P:], 0.0)
            dve.memset(ps_z[1], 0.0)
            dve.wait_ge(consts_set, 5)
            dve.tensor_copy(iota, iota_sb[:, :]).then_inc(edge_ready, 1)
            dve.wait_ge(edge_ready, 1)
            dve.sem_inc(onehot_set, LEAD - 1)
            dve.sem_inc(z_added, LEAD - 2)
            dve.sem_inc(score_set, LEAD - 2)
            dve.wait_ge(aggr_begun, STEPS)
            dve.sem_inc(aggr_set, LEAD - 3)

            def score_group(at, k):
                dve.wait_ge(groups_ready, at(k))
                dve.wait_ge(z_psum, at(k))
                add_a(dve, k % 2, k % SLOTS).then_inc(z_added, 1)
                dve.wait_ge(z_added, at(k))
                score_edges(dve, k % 2).then_inc(score_set, 1)

            def add_group(at, k, group):
                first = dve.value_load(first_row[0:1, ds(group + LAG, 1)], min_val=0, max_val=BIG)
                dve.wait_ge(sum_psum, at(k))
                dve.wait_ge(aggr_set, at(k - 1))
                add_sums(dve, k % 2, first).then_inc(aggr_set, 1)

            with dve.Fori(0, ROUNDS) as r:
                at = counts(dve, r)
                for k in range(SLOTS):
                    dve.wait_ge(weighted_set, at(k - 4))
                    spread_onehot(dve, dst_in[:, ds(r * (SLOTS * TILES) + k * TILES, TILES)], onehot[:, k % 4]).then_inc(onehot_set, 1)
                    score_group(at, k - 1)
                    add_group(at, k - 2, r * SLOTS + (k - 2))
            tail = lambda k: GROUPS + k + LEAD
            score_group(tail, -1)
            add_group(tail, -2, GROUPS - 2)
            add_group(tail, -1, GROUPS - 1)
            dve.wait_ge(aggr_set, tail(-1))
            dve.sem_inc(edges_done, 1)

            any_more = dve.value_load(most_more[0:1, 0:1], min_val=0, max_val=BLOCKS)
            with dve.If(any_more > 0):
                done = dve.alloc_register("dve_done")
                dve.reg_mov(done, 1)
                with dve.Fori(0, GROUPS) as g:
                    first = dve.value_load(first_row[0:1, ds(g + LAG, 1)], min_val=0, max_val=BIG)
                    last = dve.value_load(last_window[0:1, ds(g, 1)], min_val=2, max_val=BLOCKS)
                    with dve.Fori(1, last) as w:
                        n = dve.snap(done, min_val=1, max_val=GROUPS * BLOCKS)
                        dve.tensor_scalar(shifted[:, :], dst_in[:, ds(g * TILES, TILES)], shifts[:, ds(w, 1)], None, ALU.subtract).then_inc(more["shifted"], 1)
                        dve.wait_ge(more["shifted"], n)
                        spread_onehot(dve, shifted[:, :], onehot[:, 0]).then_inc(more["onehot"], 1)
                        dve.wait_ge(more["z_psum"], n)
                        dve.wait_ge(more["gathered"], (g + 1) * (16 * TILES))
                        add_a(dve, 0, 0).then_inc(more["z_added"], 1)
                        dve.wait_ge(more["z_added"], n)
                        score_edges(dve, 0).then_inc(more["score"], 1)
                        dve.wait_ge(more["sum_psum"], n)
                        at_node = dve.snap((first + w * P).with_bounds(min_val=0, max_val=BIG + P))
                        add_sums(dve, 0, at_node).then_inc(more["aggr"], 1)
                        dve.wait_ge(more["aggr"], n + 1)
                        dve.reg_add(done, done, 1)
            dve.sem_inc(all_done, 1)

            def mix(i):
                dve.wait_ge(gated_psum, i + 1)
                dve.tensor_tensor(at_step(h_all, i), at_step(h_all, i), grid(ps_mix[i % 2]), ALU.add).then_inc(mixed, 1)

            for i in range(STEPS):
                dve.wait_ge(gate_set, i + 1)
                dve.tensor_tensor(columns(gates, i), columns(gates, i), columns(aggrT, i), ALU.mult).then_inc(gated, 1)
                if i:
                    mix(i - 1)
                if i == STEPS - 1:
                    dve.wait_ge(sd2_set, 1)
                    reciprocals(0, SPLIT * STEP, shift2_set, STEPS)
                if i:
                    dve.wait_ge(mixed, i)
                    statistics(i - 1, mv2_set, STEPS + i - 1)
            mix(STEPS - 1)
            dve.wait_ge(mixed, STEPS)
            statistics(STEPS - 1, mv2_set, 2 * STEPS - 1)
            dve.wait_ge(sd2_set, 2)
            reciprocals(SPLIT * STEP, BLOCKS, shift2_set, STEPS + 1)
            dve.wait_ge(params_in, 16 * PARAMS)
            for turn in range(STEPS + 2):
                if turn < STEPS:
                    dve.wait_ge(normed2, turn + 1)
                    dve.tensor_tensor(at_step(h_all, turn), at_step(h_all, turn), step_bc(g2_bc), ALU.mult).then_inc(scaled2, 1)
                if turn >= 2:
                    i = turn - 2
                    dve.wait_ge(sd3_set, i + 1)
                    reciprocals(i * STEP, (i + 1) * STEP, shift3_set, STEPS + 2 + i)
                    normalise(i, OUT_PART, out_rest_set)
                if 1 <= turn <= STEPS:
                    dve.wait_ge(y_set, turn)
                    statistics(turn - 1, mv3_set, 2 * STEPS + turn - 1)


_INS = ["x", "src", "dst", "L0_gnn_W1", "L0_gnn_b1", "L0_gnn_g1", "L0_gnn_bt1", "L0_gnn_We1", "L0_gnn_be1", "L0_gnn_We2",
        "L0_gnn_be2", "L0_gnn_Wg", "L0_gnn_bg", "L0_gnn_g2", "L0_gnn_bt2"]


def kernel(**inputs):
    import numpy as _np
    import concourse.bacc as _bacc
    from concourse import mybir as _mybir
    from concourse.bass_utils import run_bass_kernel_spmd as _run

    nc = _bacc.Bacc("TRN2", target_bir_lowering=False, num_devices=1)
    arrays, args = {}, []
    for name in _INS:
        a = _np.ascontiguousarray(inputs[name])
        arrays[f"in_{name}_dram"] = a
        args.append(nc.dram_tensor(f"in_{name}_dram", a.shape, _mybir.dt.from_np(a.dtype), kind="ExternalInput").ap())
    args.append(nc.dram_tensor("out_0_dram", arrays["in_x_dram"].shape, _mybir.dt.float32, kind="ExternalOutput").ap())
    gnn_layer(nc, *args)
    r = _run(nc, [arrays], core_ids=[0])
    return r.results[0]["out_0_dram"]
```
